# Optimizing a Trainium2 kernel written in Bass

```python
import numpy as np
import jax
import jax.numpy as jnp

def _softmax(x, axis=-1):
    return jax.nn.softmax(x, axis=axis)

def _gelu(x):
    return jax.nn.gelu(x, approximate=True)

def _silu(x):
    return jax.nn.silu(x)

def _sigmoid(x):
    return jax.nn.sigmoid(x)

def _layernorm(x, axis=-1, eps=1e-05):
    m = jnp.mean(x, axis=axis, keepdims=True)
    v = jnp.var(x, axis=axis, keepdims=True)
    return (x - m) / jnp.sqrt(v + eps)

def _scatter_add(tgt, idx, src, axis=0):
    return tgt.at[idx].add(src)

def _segment_sum(src, seg, n):
    return jax.ops.segment_sum(src, seg, n)
kernel_name = 'mk_gnn_resnorm_d4_gnn_r8_646488'

def setup_inputs(seed: int=0):
    np.random.seed(seed)
    _w = jnp.asarray

    def _rec_inputs():
        import jax
        import jax.numpy as jnp
        _gk = jax.random.key(seed)
        x = -0.0005207 + 1.001 * jax.random.normal(jax.random.fold_in(_gk, 1), (8192, 32), jnp.float32)
        src = jax.random.randint(jax.random.fold_in(_gk, 2), (262144,), 0, 8192, jnp.int32)
        dst = jax.random.randint(jax.random.fold_in(_gk, 3), (262144,), 0, 8192, jnp.int32)
        _o = jnp.argsort(dst, stable=True)
        src = src[_o]
        dst = dst[_o]
        edge_attr_32 = 0.000216709 + 1.00012 * jax.random.normal(jax.random.fold_in(_gk, 12), (262144, 32), jnp.float32)
        edge_attr_4 = 0.000714719 + 1.00021 * jax.random.normal(jax.random.fold_in(_gk, 13), (262144, 4), jnp.float32)
        edge_type_64 = jax.random.randint(jax.random.fold_in(_gk, 15), (262144,), 0, 64, jnp.int32)
        edge_weight = 0.000452788 + 0.999756 * jax.random.normal(jax.random.fold_in(_gk, 16), (262144,), jnp.float32)
        return (x, src, dst, edge_attr_32, edge_attr_4, edge_type_64, edge_weight)
    x, src, dst, edge_attr_32, edge_attr_4, edge_type_64, edge_weight = _rec_inputs()

    def _L0_gnn_setup():
        import jax, jax.numpy as jnp
        import numpy as np
        N_NODES = 8192
        N_EDGES = 32768
        IN_FEAT = 32
        OUT_FEAT = 32
        NUM_RELS = 64
        key = jax.random.key(seed)
        k1, k2, k3, k4, k5 = jax.random.split(key, 5)
        feat = jax.random.normal(k1, (N_NODES, IN_FEAT), dtype=jnp.float32)
        weight = jax.random.normal(k2, (NUM_RELS, IN_FEAT, OUT_FEAT), dtype=jnp.float32)
        src = jax.random.randint(k3, (N_EDGES,), 0, N_NODES, dtype=jnp.int32)
        dst = jax.random.randint(k4, (N_EDGES,), 0, N_NODES, dtype=jnp.int32)
        etypes = jax.random.randint(k5, (N_EDGES,), 0, NUM_RELS, dtype=jnp.int32)
        return {'feat': feat, 'weight': weight, 'src': src, 'dst': dst, 'etypes': etypes}
    _L0_gnn_all = _L0_gnn_setup()
    _L0_gnn_in = {k: v for k, v in _L0_gnn_all.items() if k in ('weight',)}
    del _L0_gnn_all

    def _L1_gnn_setup():
        import jax, jax.numpy as jnp
        import numpy as np
        N_NODES = 12500
        N_EDGES = 200000
        D_FEAT = 32
        key = jax.random.key(seed)
        k1, k2, k3 = jax.random.split(key, 3)
        x = jax.random.normal(k1, (N_NODES, D_FEAT), dtype=jnp.float32)
        a = jax.random.randint(k2, (2, N_EDGES), 0, N_NODES, dtype=jnp.int64)
        e = jax.random.normal(k3, (N_EDGES,), dtype=jnp.float32)
        return {'x': x, 'a': a, 'e': e}
    _L1_gnn_all = _L1_gnn_setup()
    _L1_gnn_in = {k: v for k, v in _L1_gnn_all.items() if k in ()}
    del _L1_gnn_all

    def _L2_gnn_setup():
        import jax, jax.numpy as jnp
        import numpy as np
        N_NODES = 12500
        N_EDGES = 200000
        D_FEAT = 32
        key = jax.random.key(seed)
        kx, ke = jax.random.split(key)
        x = jax.random.normal(kx, (N_NODES, D_FEAT), dtype=jnp.float32)
        edge_index = jax.random.randint(ke, (2, N_EDGES), 0, N_NODES, dtype=jnp.int64)
        return {'x': x, 'edge_index': edge_index}
    _L2_gnn_all = _L2_gnn_setup()
    _L2_gnn_in = {k: v for k, v in _L2_gnn_all.items() if k in ()}
    del _L2_gnn_all

    def _L3_gnn_setup():
        import jax, jax.numpy as jnp
        import numpy as np
        MUL = 8
        N_NODES = 12500
        N_EDGES = 100000
        EDGE_DIM = 32
        MLP_DIM = 64
        W_NUMEL = 4 * MUL * MUL
        ALPHA = 0.25
        C110 = 1.0 / np.sqrt(3.0)
        SI_SCALE = 1.0 / np.sqrt(MUL)
        key = jax.random.key(seed)
        ks = jax.random.split(key, 10)
        node_attr = jax.random.normal(ks[0], (N_NODES, 4 * MUL), dtype=jnp.float32)
        edge_index = jax.random.randint(ks[1], (2, N_EDGES), 0, N_NODES, dtype=jnp.int64)
        edge_sh = jax.random.normal(ks[2], (N_EDGES, 4), dtype=jnp.float32)
        edge_feat = jax.random.normal(ks[3], (N_EDGES, EDGE_DIM), dtype=jnp.float32)
        W1 = jax.random.normal(ks[4], (EDGE_DIM, MLP_DIM), dtype=jnp.float32) / np.sqrt(EDGE_DIM)
        b1 = jnp.zeros((MLP_DIM,), dtype=jnp.float32)
        W2 = jax.random.normal(ks[5], (MLP_DIM, W_NUMEL), dtype=jnp.float32) / np.sqrt(MLP_DIM)
        b2 = jnp.zeros((W_NUMEL,), dtype=jnp.float32)
        si_w0 = jax.random.normal(ks[6], (MUL, MUL), dtype=jnp.float32)
        si_w1 = jax.random.normal(ks[7], (MUL, MUL), dtype=jnp.float32)
        return {'node_attr': node_attr, 'edge_index': edge_index, 'edge_sh': edge_sh, 'edge_feat': edge_feat, 'W1': W1, 'b1': b1, 'W2': W2, 'b2': b2, 'si_w0': si_w0, 'si_w1': si_w1}
    _L3_gnn_all = _L3_gnn_setup()
    _L3_gnn_in = {k: v for k, v in _L3_gnn_all.items() if k in ('W1', 'b1', 'W2', 'b2', 'si_w0', 'si_w1')}
    del _L3_gnn_all
    return {'x': x, 'src': src, 'dst': dst, 'edge_attr_32': edge_attr_32, 'edge_attr_4': edge_attr_4, 'edge_type_64': edge_type_64, 'edge_weight': edge_weight, 'L0_gnn_weight': _L0_gnn_in['weight'], 'L3_gnn_W1': _L3_gnn_in['W1'], 'L3_gnn_b1': _L3_gnn_in['b1'], 'L3_gnn_W2': _L3_gnn_in['W2'], 'L3_gnn_b2': _L3_gnn_in['b2'], 'L3_gnn_si_w0': _L3_gnn_in['si_w0'], 'L3_gnn_si_w1': _L3_gnn_in['si_w1']}

def reference(x, src, dst, edge_attr_32, edge_attr_4, edge_type_64, edge_weight, L0_gnn_weight, L3_gnn_W1, L3_gnn_b1, L3_gnn_W2, L3_gnn_b2, L3_gnn_si_w0, L3_gnn_si_w1):
    import jax
    import jax.numpy as jnp

    def _L0_gnn_ref(feat, weight, src, dst, etypes):
        import jax, jax.numpy as jnp
        import numpy as np
        N_NODES = 8192
        N_EDGES = 32768
        IN_FEAT = 32
        OUT_FEAT = 32
        NUM_RELS = 64
        w_e = jnp.take(weight, etypes, axis=0)
        h_src = jnp.take(feat, src, axis=0)
        msg = jnp.einsum('ei,eio->eo', h_src, w_e)
        out = jax.ops.segment_sum(msg, dst, num_segments=N_NODES)
        return out

    def _L1_gnn_ref(x, a, e):
        import jax, jax.numpy as jnp
        import numpy as np
        N_NODES = 12500
        N_EDGES = 200000
        D_FEAT = 32
        src = a[0]
        tgt = a[1]
        msgs = x[src] * e[:, None]
        out = jax.ops.segment_sum(msgs, tgt, num_segments=x.shape[0])
        return out

    def _L2_gnn_ref(x, edge_index):
        import jax, jax.numpy as jnp
        import numpy as np
        N_NODES = 12500
        N_EDGES = 200000
        D_FEAT = 32
        src = edge_index[0]
        dst = edge_index[1]
        msgs = jnp.take(x, src, axis=0)
        out = jax.ops.segment_sum(msgs, dst, num_segments=x.shape[0])
        return out

    def _L3_gnn_ref(node_attr, edge_index, edge_sh, edge_feat, W1, b1, W2, b2, si_w0, si_w1):
        import jax, jax.numpy as jnp
        import numpy as np
        MUL = 8
        N_NODES = 12500
        N_EDGES = 100000
        EDGE_DIM = 32
        MLP_DIM = 64
        W_NUMEL = 4 * MUL * MUL
        ALPHA = 0.25
        C110 = 1.0 / np.sqrt(3.0)
        SI_SCALE = 1.0 / np.sqrt(MUL)
        n = node_attr.shape[0]
        e = edge_sh.shape[0]
        h = jax.nn.relu(edge_feat @ W1 + b1)
        w = (h @ W2 + b2).reshape(e, 4, MUL, MUL)
        w_000, w_011, w_101, w_110 = (w[:, 0], w[:, 1], w[:, 2], w[:, 3])
        s = node_attr[:, :MUL]
        v = node_attr[:, MUL:].reshape(n, MUL, 3)
        src, dst = (edge_index[0], edge_index[1])
        s_e = s[src]
        v_e = v[src]
        sh0 = edge_sh[:, 0]
        sh1 = edge_sh[:, 1:4]
        m0 = ALPHA * (jnp.einsum('ei,eio->eo', s_e * sh0[:, None], w_000) + C110 * jnp.einsum('eim,em,eio->eo', v_e, sh1, w_110))
        m1 = ALPHA * (jnp.einsum('ei,em,eio->eom', s_e, sh1, w_011) + jnp.einsum('eim,eio->eom', v_e * sh0[:, None, None], w_101))
        out0 = jax.ops.segment_sum(m0, dst, num_segments=n)
        out1 = jax.ops.segment_sum(m1.reshape(e, MUL * 3), dst, num_segments=n).reshape(n, MUL, 3)
        out0 = out0 + SI_SCALE * (s @ si_w0)
        out1 = out1 + SI_SCALE * jnp.einsum('nim,io->nom', v, si_w1)
        return jnp.concatenate([out0, out1.reshape(n, MUL * 3)], axis=-1)
    edge_index = jnp.stack([src, dst])
    x = _layernorm(x + _L0_gnn_ref(x, L0_gnn_weight, src, dst, edge_type_64), axis=-1)
    x = _layernorm(x + _L1_gnn_ref(x, edge_index, edge_weight), axis=-1)
    x = _layernorm(x + _L2_gnn_ref(x, edge_index), axis=-1)
    x = _layernorm(x + _L3_gnn_ref(x, edge_index, edge_attr_4, edge_attr_32, L3_gnn_W1, L3_gnn_b1, L3_gnn_W2, L3_gnn_b2, L3_gnn_si_w0, L3_gnn_si_w1), axis=-1)
    return x

_drawn_inputs = setup_inputs


def setup_inputs(seed=0):
    import zlib

    import numpy as np

    out = dict(_drawn_inputs(seed))
    spreads = {'L3_gnn_b1': (0.0, 0.1), 'L3_gnn_b2': (0.0, 0.1)}
    factors = {}
    for name, (base, spread) in spreads.items():
        noise = np.random.default_rng([zlib.crc32(name.encode()), seed]).standard_normal(out[name].shape)
        drawn = base * np.exp(spread * noise) if base else spread * noise
        out[name] = jnp.asarray(drawn.astype(out[name].dtype))
    for name, factor in factors.items():
        out[name] = (out[name] * factor).astype(out[name].dtype)
    return out
```

```python
from contextlib import ExitStack

import concourse.bass as bass
from concourse import mybir

P = 128
F = 32
TILES = 16
CHUNK = TILES * P
FIRST = 0
SLOTS = 4
GROUP = 4
MUL = 8
HALF = 1024

ALU = mybir.AluOpType
ACT = mybir.ActivationFunctionType
F32 = mybir.dt.float32
I32 = mybir.dt.int32
AX = mybir.AxisListType
ALPHA = 0.25
C110 = 3.0 ** -0.5
SI_SCALE = MUL ** -0.5
HID = 64
WN = 4 * MUL * MUL
A_END = 2 * MUL * MUL
Q_END = 3 * MUL * MUL
MA = MUL * MUL
MQ = MA + 3 * MUL
MSG = MQ + 3 * MUL * 4
ZC = 2 * MUL
SETUP_MINMAX = 8
SETUP_COL = 10
SETUP_ROW = 11


def build(nc, x, src, dst, edge_attr_32, edge_attr_4, edge_type_64, edge_weight, L0_gnn_weight,
          L3_gnn_W1, L3_gnn_b1, L3_gnn_W2, L3_gnn_b2, L3_gnn_si_w0, L3_gnn_si_w1, out):
    NODES = x.shape[0]
    EDGES = src.shape[0]
    RELS = L0_gnn_weight.shape[0]
    BLOCKS = NODES // P
    CHUNKS = EDGES // CHUNK
    COLS = CHUNKS * TILES
    ROUNDS = CHUNKS // SLOTS
    assert CHUNKS == P and BLOCKS % 4 == 0 and RELS * F == 2 * HALF

    with ExitStack() as ctx:
        def sb(name, shape, dt=F32):
            return ctx.enter_context(nc.sbuf_tensor(name, shape, dt))

        def sem(name):
            return ctx.enter_context(nc.semaphore(name))

        rel_table = nc.dram_tensor("rel_table", [NODES * RELS, F], F32).ap()
        rows = [rel_table] + [nc.dram_tensor(f"x_rows_{n}", [NODES, F], F32).ap() for n in (1, 2, 3)]

        src_i = sb("src_i", [P, COLS], I32)
        dst_i = sb("dst_i", [P, COLS], I32)
        key_i = sb("key_i", [P, COLS], I32)
        dst_f = sb("dst_f", [P, COLS])
        dmod_i = sb("dmod_i", [P, COLS], I32)
        dmod1 = sb("dmod1", [P, COLS])
        weight = sb("weight", [P, COLS])

        dst_min = sb("dst_min", [P, CHUNKS])
        dst_max = sb("dst_max", [P, CHUNKS])
        col_min = sb("col_min", [P, 2])
        row_min = sb("row_min", [1, 2, CHUNKS])
        row_i = sb("row_i", [1, 2, CHUNKS], I32)
        meta = sb("meta", [1, 3, CHUNKS], I32)
        base = sb("base", [P, CHUNKS])
        base_i = sb("base_i", [P, CHUNKS], I32)
        basemod = sb("basemod", [P, CHUNKS])
        in_first = sb("in_first", [P, CHUNKS])
        in_next = sb("in_next", [P, CHUNKS])

        iota_i = sb("iota_i", [P, P], I32)
        iota1 = sb("iota1", [P, P])
        part_i = sb("part_i", [P, 1], I32)
        part = sb("part", [P, 1])
        part1 = sb("part1", [P, 1])
        ident = sb("ident", [P, P])
        ones = sb("ones", [1, P])
        epsc = sb("epsc", [P, 1])

        rel_w = sb("rel_w", [P, RELS * F])
        group_x = sb("group_x", [P, P])
        group_xT = sb("group_xT", [P, P])
        table_out = sb("table_out", [P, 2, RELS * F])

        idx = sb("idx", [P, SLOTS, TILES], I32)
        gathered = sb("gathered", [P, SLOTS, TILES, F])
        onehot = sb("onehot", [P, 2, TILES, P])
        window = sb("window", [P, 1])
        window_end = sb("window_end", [P, 1])
        reached = sb("reached", [P, TILES])
        key = sb("key", [P, TILES])

        w1 = sb("w1", [P, HID + 1])
        bias1 = sb("bias1", [HID + 1, 1])
        w2_raw = sb("w2_raw", [HID + 1, WN])
        w2 = sb("w2", [HID + 1, WN])
        w_self = sb("w_self", [P, F])
        edge_in = sb("edge_in", [P, SLOTS, TILES, F])
        sh = sb("sh", [P, SLOTS, TILES, 4])
        edge_T = sb("edge_T", [P, GROUP * P])
        hidden = sb("hidden", [HID + 1, 2, GROUP, GROUP * P])
        z = sb("z", [P, 2, TILES, 5 * MUL])
        cprod = sb("cprod", [P, TILES, MUL, 3])
        prod_a = sb("prod_a", [P, GROUP, MUL, 2 * MUL])
        prod_q = sb("prod_q", [P, GROUP, MUL, MUL])
        prod_v = sb("prod_v", [P, GROUP, 3, MUL, MUL])
        q_sum = sb("q_sum", [P, GROUP, MUL])
        msg = sb("msg", [P, 2, TILES, MSG])
        folded = sb("folded", [P, F])
        folded_q = sb("folded_q", [P, 3 * MUL])

        xn = sb("xn", [P, BLOCKS, F])
        acc = sb("acc", [P, BLOCKS + 1, F])
        cen = table_out[:, 0, :].rearrange("p (b f) -> p b f", f=F)
        sq = table_out[:, 1, :].rearrange("p (b f) -> p b f", f=F)
        st1 = sb("st1", [P, BLOCKS])
        st2 = sb("st2", [P, BLOCKS])
        st3 = sb("st3", [P, BLOCKS])

        psum = ctx.enter_context(nc.psum_tensor("psum", [P, 8, 512], F32))
        pair = [psum[:, 2 * k:2 * k + 2, :].rearrange("p a b -> p (a b)") for k in range(2)]
        bank_t = psum[:, 4, :]
        bank_h = [psum[:, 5, :], psum[:, 6, :]]
        bank_s = psum[:, 7, :]

        loaded = sem("loaded")
        x_loaded = sem("x_loaded")
        rel_loaded = sem("rel_loaded")
        iota_done = sem("iota_done")
        setup = sem("setup")
        ident_done = sem("ident_done")
        turned = sem("turned")
        keys_ready = sem("keys_ready")
        meta_ready = sem("meta_ready")
        x_staged = sem("x_staged")
        x_turned = sem("x_turned")
        xT_ready = sem("xT_ready")
        table_mm = sem("table_mm")
        evac_a = sem("evac_a")
        evac_v = sem("evac_v")
        table_stored = [sem("table_stored_0"), sem("table_stored_1")]
        rows_in = [[sem(f"rows_in_{l}_{s}") for s in range(SLOTS)] for l in range(4)]
        window_set = sem("window_set")
        window_moved = sem("window_moved")
        reached_ready = sem("reached_ready")
        key_ready = sem("key_ready")
        onehot_ready = sem("onehot_ready")
        scattered = sem("scattered")
        added = sem("added")
        slot_freed = sem("slot_freed")
        sq_done = sem("sq_done")
        std_done = sem("std_done")
        x_ready = sem("x_ready")
        rows_out = [sem(f"rows_out_{l}") for l in range(4)]
        idx_in = [sem(f"idx_in_{s}") for s in range(SLOTS)]
        zeroed = sem("zeroed")
        w3_loaded = sem("w3_loaded")
        w3_ready = sem("w3_ready")
        self_made = sem("self_made")
        self_added = sem("self_added")
        edges_in = [sem(f"edges_in_{s}") for s in range(SLOTS)]
        edges_turned = sem("edges_turned")
        edge_T_ready = sem("edge_T_ready")
        hidden_made = sem("hidden_made")
        hidden_ready = sem("hidden_ready")
        z_scaled = sem("z_scaled")
        z_free = sem("z_free")
        w_made = sem("w_made")
        pair_free = sem("pair_free")
        cprod_ready = sem("cprod_ready")
        c_ready = sem("c_ready")
        products = sem("products")
        q_ready = sem("q_ready")
        folds = sem("folds")
        msg_ready = sem("msg_ready")
        onehot3_ready = sem("onehot3_ready")
        key3_ready = sem("key3_ready")
        reach3_ready = sem("reach3_ready")
        window3_ready = sem("window3_ready")
        scattered3 = sem("scattered3")
        folded_ready = sem("folded_ready")
        added3 = sem("added3")
        extra = {n: sem("extra_" + n) for n in ("window", "moved", "reached", "key", "onehot", "scattered",
                                                 "fold", "folded", "added")}

        edge_cols = lambda a: a.rearrange("(c p j) -> p c j", p=P, j=TILES)
        node_rows = lambda a: a.rearrange("(b p) f -> p b f", p=P)
        cols3 = lambda t: t[:, :].rearrange("p (c j) -> p c j", j=TILES)

        edge_rows = edge_attr_32.rearrange("(c p j) f -> c p (j f)", p=P, j=TILES)
        sh_rows = edge_attr_4.rearrange("(c p j) f -> c p (j f)", p=P, j=TILES)
        W3_LOADS = 16 * (4 * 5 + 3)

        block = ctx.enter_context(nc.Block())

        @block.sync
        def _(sp):
            sp.dma_start(xn[:, :, :], node_rows(x)).then_inc(x_loaded, 16)
            for q in range(4):
                sp.dma_start(rel_w[F * q:F * q + F, :].rearrange("i (r o) -> i r o", o=F),
                             L0_gnn_weight.rearrange("r i o -> i r o")).then_inc(rel_loaded, 16)
            sp.dma_start(cols3(dst_i), edge_cols(dst)).then_inc(loaded, 16)
            sp.dma_start(cols3(src_i), edge_cols(src)).then_inc(loaded, 16)
            sp.dma_start(cols3(key_i), edge_cols(edge_type_64)).then_inc(loaded, 16)
            sp.dma_start(cols3(weight), edge_cols(edge_weight)).then_inc(loaded, 16)

            sp.wait_ge(zeroed, 1)
            for q in range(4):
                sp.dma_start(w1[F * q:F * q + F, 0:HID], L3_gnn_W1).then_inc(w3_loaded, 16)
                sp.dma_start(w_self[F * q:F * q + MUL, 0:MUL], L3_gnn_si_w0).then_inc(w3_loaded, 16)
                for m in range(3):
                    sp.dma_start(w_self[F * q + MUL + m:F * q + F:3, MUL + m:F:3], L3_gnn_si_w1, allow_slow_non_contiguous=True
                                 ).then_inc(w3_loaded, 16)
            sp.dma_start(bias1[0:HID, :], L3_gnn_b1.rearrange("(h a) -> h a", a=1)).then_inc(w3_loaded, 16)
            sp.dma_start(w2_raw[0:HID, :], L3_gnn_W2).then_inc(w3_loaded, 16)
            sp.dma_start(w2_raw[HID:HID + 1, :], L3_gnn_b2.rearrange("(a n) -> a n", a=1)).then_inc(w3_loaded, 16)

            table_rows = rel_table.rearrange("(b p r) o -> b p (r o)", p=P, r=RELS)
            with sp.Fori(0, BLOCKS // 2) as it:
                for h in range(2):
                    sp.wait_ge(evac_a, it * 2 + (h + 1))
                    sp.wait_ge(evac_v, it * 2 + (h + 1))
                    sp.dma_start(table_rows[bass.ds(it * 2 + h, 1), :, :].rearrange("b p c -> p (b c)"),
                                 table_out[:, h, :]).then_inc(table_stored[h], 16)

            sp.wait_ge(keys_ready, 1)
            for l in range(4):
                numbers = key_i if l == 0 else src_i
                with sp.Fori(0, ROUNDS) as it:
                    for s in range(SLOTS):
                        c = it * SLOTS + s
                        sp.wait_ge(slot_freed, it * SLOTS + (l * CHUNKS + s + 1))
                        sp.dma_start(idx[:, s, :], numbers[:, bass.ds(it * (SLOTS * TILES) + s * TILES, TILES)]
                                     ).then_inc(idx_in[s], 16)
                        if l == 3:
                            sp.dma_start(edge_in[:, s, :, :].rearrange("p j f -> p (j f)"),
                                         edge_rows[bass.ds(c, 1), :, :].rearrange("c p k -> p (c k)")
                                         ).then_inc(edges_in[s], 16)
                            sp.dma_start(sh[:, s, :, :].rearrange("p j f -> p (j f)"),
                                         sh_rows[bass.ds(c, 1), :, :].rearrange("c p k -> p (c k)")
                                         ).then_inc(edges_in[s], 16)

        @block.gpsimd
        def _(pool):
            pool.iota(iota_i[:, :], [[1, P]], base=1, channel_multiplier=0).then_inc(iota_done, 1)
            pool.iota(part_i[:, :], [[1, 1]], base=0, channel_multiplier=1).then_inc(iota_done, 1)
            for s in table_stored:
                pool.wait_ge(s, 16 * (BLOCKS // 2))
            due = [pool.alloc_register(f"idx_due_{s}") for s in range(SLOTS)]
            for s in range(SLOTS):
                pool.reg_mov(due[s], 16)
            for l in range(4):
                if l >= 1:
                    pool.wait_ge(rows_out[l - 1], 16)
                with pool.Fori(0, ROUNDS) as it:
                    for s in range(SLOTS):
                        pool.wait_ge(idx_in[s], pool.snap(due[s]))
                        pool.reg_add(due[s], due[s], 16)
                        for j in range(TILES):
                            pool.indirect_dma_start(
                                gathered[:, s, j, :], None, rows[l],
                                bass.IndirectOffsetOnAxis(ap=idx[:, s, j:j + 1], axis=0),
                            ).then_inc(rows_in[l][s], 16)

        @block.scalar
        def _(act):
            def table_group(g):
                if g is not FIRST:
                    act.wait_ge(x_turned, g)
                act.copy(group_x[:, :], xn[:, bass.ds(g * 4, 4), :].rearrange("p b f -> p (b f)")
                         ).then_inc(x_staged, 1)
                act.wait_ge(x_turned, g + 1)
                if g is not FIRST:
                    act.wait_ge(table_mm, g * 8)
                act.copy(group_xT[:, :], bank_t[:, 0:P]).then_inc(xT_ready, 1)
                for q in range(4):
                    h = q % 2
                    act.wait_ge(table_mm, g * 8 + (2 * q + 1))
                    if g is not FIRST or q >= 2:
                        act.wait_ge(table_stored[h], g * 32 + 16 * (q // 2))
                    act.copy(table_out[:, h, 0:HALF], pair[0]).then_inc(evac_a, 1)

            act.wait_ge(x_loaded, 16)
            table_group(FIRST)
            with act.Fori(1, BLOCKS // 4) as g:
                table_group(g)

            def normalise(l):
                act.wait_ge(sq_done, 2 * l + 1)
                act.activation(sq[:, :, :], cen[:, :, :], ACT.Square).then_inc(sq_done, 1)
                act.wait_ge(std_done, 2 * l + 1)
                act.activation(st2[:, :], st1[:, :], ACT.Sqrt, bias=epsc[:, :], scale=1.0 / F).then_inc(std_done, 1)
                act.wait_ge(x_ready, l + 1)
                act.dma_start(node_rows(out if l == 3 else rows[l + 1]), xn[:, :, :]).then_inc(rows_out[l], 16)

            for l in range(3):
                normalise(l)

            with act.Fori(0, BLOCKS // 4) as g:
                act.wait_ge(x_turned, g + BLOCKS // 4)
                act.copy(group_x[:, :], xn[:, bass.ds(g * 4, 4), :].rearrange("p b f -> p (b f)")
                         ).then_inc(x_staged, 1)
                act.wait_ge(x_turned, g + (BLOCKS // 4 + 1))
                act.wait_ge(self_made, g + 1)
                act.copy(group_xT[:, :], bank_t[:, 0:P]).then_inc(xT_ready, 1)

            def hidden_units(c, s):
                act.wait_ge(edges_turned, c + 1)
                act.wait_ge(hidden_made, c * GROUP + 1)
                act.copy(edge_T[:, :], bank_t).then_inc(edge_T_ready, 1)
                for q in range(GROUP):
                    act.wait_ge(hidden_made, c * GROUP + (q + 2))
                    if q == 0:
                        act.wait_ge(w_made, c * GROUP + GROUP)
                    act.activation(hidden[:, s % 2, q, :], bank_h[q % 2][0:HID + 1, :], ACT.Relu,
                                   bias=bias1[:, :]).then_inc(hidden_ready, 1)

            def scale_rows(c, s, it):
                act.wait_ge(rows_in[3][s], it * (16 * TILES) + 16 * TILES)
                act.wait_ge(edges_in[s], it * 32 + 32)
                act.wait_ge(z_free, c + 1)
                for j in range(TILES):
                    a = act.activation(z[:, s % 2, j, MUL:], gathered[:, s, j, :], ACT.Copy,
                                       scale=sh[:, s, j, 0:1])
                a.then_inc(z_scaled, 1)

            act.wait_ge(w3_ready, 1)
            hidden_units(0, 0)
            with act.Fori(0, ROUNDS - 1) as it:
                for s in range(SLOTS):
                    scale_rows(it * SLOTS + s, s, it)
                    hidden_units(it * SLOTS + (s + 1), s + 1)
            for s in range(SLOTS):
                c = CHUNKS - SLOTS + s
                scale_rows(c, s, ROUNDS - 1)
                if c + 1 < CHUNKS:
                    hidden_units(c + 1, s + 1)
            normalise(3)
            act.wait_ge(rows_out[3], 16)

        @block.tensor
        def _(pe):
            pe.wait_ge(setup, SETUP_MINMAX)
            pe.wait_ge(ident_done, 1)
            pe.transpose(psum[:, 5, 0:P], dst_min[:, :], ident[:, :]).then_inc(turned, 1)
            pe.transpose(psum[:, 6, 0:P], dst_max[:, :], ident[:, :]).then_inc(turned, 1)
            pe.wait_ge(setup, SETUP_COL)
            pe.transpose(psum[0:1, 5, 0:P], col_min[:, 0:1], ident[:, :]).then_inc(turned, 1)
            pe.transpose(psum[0:1, 6, 0:P], col_min[:, 1:2], ident[:, :]).then_inc(turned, 1)
            pe.wait_ge(setup, SETUP_ROW)
            pe.matmul(psum[:, 5, 0:P], ones[:, :], row_min[0:1, 0, :], start=True, stop=True).then_inc(turned, 1)

            pe.wait_ge(rel_loaded, 64)
            def table_group(g):
                pe.wait_ge(x_staged, g + 1)
                if g is not FIRST:
                    pe.wait_ge(xT_ready, g)
                pe.transpose(bank_t[:, 0:P], group_x[:, :], ident[:, :]).then_inc(x_turned, 1)
                pe.wait_ge(xT_ready, g + 1)
                for q in range(4):
                    for k in range(2):
                        if g is not FIRST or q > 0:
                            pe.wait_ge((evac_a, evac_v)[k], g * 4 + q)
                        for n in range(2):
                            mm = pe.matmul(pair[k][:, 512 * n:512 * n + 512], group_xT[F * q:F * q + F, :],
                                           rel_w[F * q:F * q + F, HALF * k + 512 * n:HALF * k + 512 * n + 512],
                                           start=True, stop=True, tile_position=(F * q, 0))
                        mm.then_inc(table_mm, 1)

            table_group(FIRST)
            with pe.Fori(1, BLOCKS // 4) as g:
                table_group(g)

            pe.wait_ge(meta_ready, 1)
            steps = pe.alloc_register("pe_steps")
            pe.reg_mov(steps, 1)
            for l in range(3):
                with pe.Fori(0, ROUNDS) as it:
                    for s in range(SLOTS):
                        first_block = pe.value_load(meta[0:1, 0, bass.ds(it * SLOTS + s, 1)], min_val=0, max_val=BLOCKS - 1)
                        end_block = pe.value_load(meta[0:1, 1, bass.ds(it * SLOTS + s, 1)], min_val=1, max_val=BLOCKS)
                        with pe.Fori(first_block, end_block):
                            step = pe.snap(steps)
                            pe.wait_ge(rows_in[l][s], it * (16 * TILES) + 16 * TILES)
                            pe.wait_ge(onehot_ready, step)
                            pe.wait_ge(added, step)
                            for j in range(TILES):
                                mm = pe.matmul(bank_s[:, 0:F], onehot[:, s % 2, j, :], gathered[:, s, j, :],
                                               start=(j == 0), stop=(j == TILES - 1))
                            mm.then_inc(scattered, 1)
                            pe.reg_add(steps, steps, 1)

            pe.wait_ge(w3_ready, 1)
            with pe.Fori(0, BLOCKS // 4) as g:
                pe.wait_ge(x_staged, g + (BLOCKS // 4 + 1))
                pe.wait_ge(xT_ready, g + BLOCKS // 4)
                pe.transpose(bank_t[:, 0:P], group_x[:, :], ident[:, :]).then_inc(x_turned, 1)
                pe.wait_ge(xT_ready, g + (BLOCKS // 4 + 1))
                pe.wait_ge(self_added, g + 1)
                for q in range(4):
                    mm = pe.matmul(psum[:, q, 0:F], group_xT[F * q:F * q + F, :], w_self[F * q:F * q + F, :],
                                   start=True, stop=True, tile_position=(F * q, 0))
                mm.then_inc(self_made, 1)
            pe.wait_ge(self_added, BLOCKS // 4 + 1)

            def turn_edges(c, s, it):
                pe.wait_ge(edges_in[s], it * 32 + 32)
                pe.wait_ge(edge_T_ready, c + 1)
                for g in range(GROUP):
                    t = pe.transpose(bank_t[:, P * g:P * g + P],
                                     edge_in[:, s, GROUP * g:GROUP * g + GROUP, :].rearrange("p j f -> p (j f)"),
                                     ident[:, :])
                t.then_inc(edges_turned, 1)

            def hidden_units(c):
                pe.wait_ge(edge_T_ready, c + 2)
                for q in range(GROUP):
                    pe.wait_ge(hidden_ready, c * GROUP + (q + 1))
                    pe.matmul(bank_h[q % 2][0:HID + 1, :], w1[F * q:F * q + F, :], edge_T[F * q:F * q + F, :],
                              start=True, stop=True, tile_position=(F * q, 0)).then_inc(hidden_made, 1)

            def edge_weights(c, s, g):
                if g == 0:
                    pe.wait_ge(hidden_ready, c * GROUP + (GROUP + 2))
                pe.wait_ge(pair_free, c * GROUP + (g + 1))
                for q in range(GROUP):
                    mm = pe.matmul(pair[g % 2][:, WN * q:WN * q + WN], hidden[:, s % 2, q, P * g:P * g + P], w2[:, :],
                                   start=True, stop=True)
                mm.then_inc(w_made, 1)

            def scatter(s, tiles):
                for j in tiles:
                    mm = pe.matmul(bank_s[:, 0:MSG], onehot[:, s % 2, j, :], msg[:, s % 2, j, :],
                                   start=(j == 0), stop=(j == TILES - 1))
                return mm

            def scatter_extra(c, s):
                first_block = pe.value_load(meta[0:1, 2, bass.ds(c, 1)], min_val=1, max_val=BLOCKS)
                end_block = pe.value_load(meta[0:1, 1, bass.ds(c, 1)], min_val=1, max_val=BLOCKS)
                with pe.If(first_block < end_block):
                    with pe.Fori(first_block, end_block):
                        n = pe.snap(extras)
                        pe.wait_ge(extra["onehot"], n + 1)
                        scatter(s, range(TILES)).then_inc(extra["scattered"], 1)
                        pe.wait_ge(extra["added"], n + 1)
                        pe.reg_add(extras, extras, 1)

            extras = pe.alloc_register("pe_extras")
            pe.reg_mov(extras, 0)

            def chunk3(c, s, it, prev=True, following=True):
                if following:
                    turn_edges(c + 1, (s + 1) % SLOTS, it if s + 1 < SLOTS else it + 1)
                for g in range(GROUP):
                    edge_weights(c, s, g)
                    if g == 0 and following:
                        hidden_units(c + 1)
                    if prev:
                        if g == 0:
                            pe.wait_ge(onehot3_ready, c)
                            pe.wait_ge(msg_ready, c * GROUP + 1)
                            pe.wait_ge(added3, c)
                        mm = scatter((s - 1) % SLOTS, range(GROUP * g, GROUP * g + GROUP))
                if prev:
                    mm.then_inc(scattered3, 1)
                    scatter_extra(c - 1, (s - 1) % SLOTS)

            turn_edges(0, 0, 0)
            hidden_units(0)
            for s in range(SLOTS):
                chunk3(s, s, 0, prev=s > 0)
            with pe.Fori(1, ROUNDS - 1) as it:
                for s in range(SLOTS):
                    chunk3(it * SLOTS + s, s, it)
            for s in range(SLOTS):
                chunk3(CHUNKS - SLOTS + s, s, ROUNDS - 1, following=s + 1 < SLOTS)
            pe.wait_ge(onehot3_ready, CHUNKS)
            pe.wait_ge(msg_ready, CHUNKS * GROUP + 1)
            pe.wait_ge(added3, CHUNKS)
            scatter(SLOTS - 1, range(TILES)).then_inc(scattered3, 1)
            scatter_extra(CHUNKS - 1, SLOTS - 1)

        @block.vector
        def _(dve):
            chain = [0]

            def link(ins):
                chain[0] += 1
                ins.then_inc(setup, 1)
                dve.wait_ge(setup, chain[0])

            dve.memset(ones[:, :], 1.0)
            dve.memset(epsc[:, :], 1e-5)
            dve.memset(acc[:, :, :], 0.0)
            dve.memset(w1[:, :], 0.0)
            dve.memset(bias1[:, :], 1.0)
            dve.memset(w_self[:, :], 0.0).then_inc(zeroed, 1)
            for start, n in ((slot_freed, SLOTS), (z_free, 2), (pair_free, 2), (hidden_ready, 2), (hidden_made, 1),
                             (edge_T_ready, 1), (self_made, 1), (self_added, 1), (added3, 1), (w_made, 2 * GROUP),
                             (msg_ready, 1), (window_moved, 1), (key_ready, 1), (scattered, 1), (added, 1),
                             (extra["moved"], 1)):
                dve.sem_inc(start, n)
            dve.wait_ge(iota_done, 2)
            link(dve.tensor_copy(iota1[:, :], iota_i[:, :]))
            link(dve.tensor_copy(part[:, :], part_i[:, :]))
            link(dve.tensor_scalar(part1[:, :], part[:, :], 1.0, None, ALU.add))
            dve.tensor_scalar(ident[:, :], iota1[:, :], part1[:, 0:1], None, ALU.is_equal).then_inc(ident_done, 1)
            dve.wait_ge(loaded, 64)
            link(dve.tensor_copy(dst_f[:, :], dst_i[:, :]))
            link(dve.tensor_scalar(dmod_i[:, :], dst_i[:, :], P - 1, None, ALU.bitwise_and))
            link(dve.tensor_scalar(dmod1[:, :], dmod_i[:, :], 1.0, None, ALU.add))
            dve.scalar_tensor_tensor(key_i[:, :], src_i[:, :], float(RELS), key_i[:, :], ALU.mult,
                                     ALU.add).then_inc(keys_ready, 1)
            link(dve.tensor_reduce(dst_min[:, :], cols3(dst_f), AX.X, ALU.min))
            link(dve.tensor_reduce(dst_max[:, :], cols3(dst_f), AX.X, ALU.max))
            assert chain[0] == SETUP_MINMAX, chain[0]
            dve.wait_ge(turned, 2)
            link(dve.tensor_reduce(col_min[:, 0:1], psum[:, 5, 0:P], AX.X, ALU.min))
            link(dve.tensor_reduce(col_min[:, 1:2], psum[:, 6, 0:P], AX.X, ALU.max))
            assert chain[0] == SETUP_COL, chain[0]
            dve.wait_ge(turned, 4)
            link(dve.tensor_copy(row_min[0:1, 0, :], psum[0:1, 5, 0:P]))
            assert chain[0] == SETUP_ROW, chain[0]
            link(dve.tensor_tensor(row_min[0:1, 1, :], psum[0:1, 6, 0:P], row_min[0:1, 0, :], ALU.subtract))
            link(dve.tensor_copy(row_i[0:1, :, :], row_min[0:1, :, :]))
            link(dve.tensor_scalar(meta[0:1, 0:2, :], row_i[0:1, :, :], 7, None, ALU.logical_shift_right))
            link(dve.scalar_tensor_tensor(meta[0:1, 1, :], meta[0:1, 1, :], 1.0, meta[0:1, 0, :], ALU.add, ALU.add))
            link(dve.tensor_scalar(meta[0:1, 2, :], meta[0:1, 0, :], 1.0, None, ALU.add))
            dve.wait_ge(turned, 5)
            link(dve.tensor_copy(base[:, :], psum[:, 5, 0:P]))
            link(dve.tensor_copy(base_i[:, :], base[:, :]))
            link(dve.tensor_scalar(base_i[:, :], base_i[:, :], P - 1, None, ALU.bitwise_and))
            link(dve.tensor_copy(basemod[:, :], base_i[:, :]))
            link(dve.tensor_scalar(in_first[:, :], basemod[:, :], part[:, 0:1], None, ALU.is_le))
            link(dve.tensor_scalar(in_next[:, :], basemod[:, :], part[:, 0:1], None, ALU.is_gt))
            dve.sem_inc(meta_ready, 1)

            dve.wait_ge(w3_loaded, W3_LOADS)
            raw = w2_raw[:, :].rearrange("h (k i o) -> h k o i", k=4, i=MUL)
            w2_a = w2[:, 0:A_END].rearrange("h (o k i) -> h k o i", o=MUL, k=2)
            oi = lambda ap: ap.rearrange("h (o i) -> h o i", o=MUL)
            dve.tensor_scalar(w2_a[:, 0], raw[:, 3], C110, None, ALU.mult)
            dve.tensor_copy(w2_a[:, 1], raw[:, 0])
            dve.tensor_copy(oi(w2[:, A_END:Q_END]), raw[:, 1])
            dve.tensor_copy(oi(w2[:, Q_END:WN]), raw[:, 2]).then_inc(w3_ready, 1)

            def normalise(l):
                if l >= 1:
                    dve.wait_ge(rows_out[l - 1], 16)
                if l == 3:
                    link(dve.scalar_tensor_tensor(xn[:, :, :], acc[:, 0:BLOCKS, :], ALPHA, xn[:, :, :],
                                                  ALU.mult, ALU.add))
                else:
                    link(dve.tensor_tensor(xn[:, :, :], xn[:, :, :], acc[:, 0:BLOCKS, :], ALU.add))
                link(dve.tensor_reduce(st1[:, :], xn[:, :, :], AX.X, ALU.add))
                link(dve.tensor_scalar(st1[:, :], st1[:, :], 1.0 / F, None, ALU.mult))
                dve.tensor_tensor(cen[:, :, :], xn[:, :, :], st1[:, :].unsqueeze(2).to_broadcast([P, BLOCKS, F]),
                                  ALU.subtract).then_inc(sq_done, 1)
                if l < 2:
                    link(dve.memset(acc[:, :, :], 0.0))
                dve.wait_ge(sq_done, 2 * l + 2)
                dve.tensor_reduce(st1[:, :], sq[:, :, :], AX.X, ALU.add).then_inc(std_done, 1)
                dve.wait_ge(std_done, 2 * l + 2)
                link(dve.reciprocal(st3[:, :], st2[:, :]))
                dve.tensor_tensor(xn[:, :, :], cen[:, :, :], st3[:, :].unsqueeze(2).to_broadcast([P, BLOCKS, F]),
                                  ALU.mult).then_inc(x_ready, 1)

            def table_group(g):
                for q in range(4):
                    h = q % 2
                    dve.wait_ge(table_mm, g * 8 + (2 * q + 2))
                    if g is not FIRST or q >= 2:
                        dve.wait_ge(table_stored[h], g * 32 + 16 * (q // 2))
                    dve.tensor_copy(table_out[:, h, HALF:2 * HALF], pair[1]).then_inc(evac_v, 1)

            table_group(FIRST)
            with dve.Fori(1, BLOCKS // 4) as g:
                table_group(g)

            steps = dve.alloc_register("dve_steps")
            dve.reg_mov(steps, 1)
            for l in range(3):
                with dve.Fori(0, ROUNDS) as it:
                    for s in range(SLOTS):
                        c = it * SLOTS + s
                        col = it * (SLOTS * TILES) + s * TILES
                        first_block = dve.value_load(meta[0:1, 0, bass.ds(c, 1)], min_val=0, max_val=BLOCKS - 1)
                        end_block = dve.value_load(meta[0:1, 1, bass.ds(c, 1)], min_val=1, max_val=BLOCKS)
                        chunk = it * SLOTS + (l * CHUNKS + s)
                        dve.wait_ge(window_moved, dve.snap(steps))
                        dve.tensor_copy(window[:, :], base[:, bass.ds(c, 1)]).then_inc(window_set, 1)
                        with dve.Fori(first_block, end_block) as b0:
                            step = dve.snap(steps)
                            dve.wait_ge(window_set, chunk + 1)
                            dve.wait_ge(window_moved, step)
                            dve.wait_ge(key_ready, step)
                            dve.scalar_tensor_tensor(reached[:, :], dst_f[:, bass.ds(col, TILES)], window[:, 0:1],
                                                     dmod1[:, bass.ds(col, TILES)], ALU.is_ge, ALU.mult
                                                     ).then_inc(reached_ready, 1)
                            dve.wait_ge(reached_ready, step)
                            dve.tensor_scalar(window[:, :], window[:, :], float(P), None, ALU.add
                                              ).then_inc(window_moved, 1)
                            dve.wait_ge(window_moved, step + 1)
                            dve.scalar_tensor_tensor(key[:, :], dst_f[:, bass.ds(col, TILES)], window[:, 0:1],
                                                     reached[:, :], ALU.is_lt, ALU.mult).then_inc(key_ready, 1)
                            dve.wait_ge(key_ready, step + 1)
                            dve.wait_ge(scattered, step)
                            for j in range(TILES):
                                if l == 1:
                                    oh = dve.tensor_scalar(onehot[:, s % 2, j, :], iota1[:, :], key[:, j:j + 1],
                                                           weight[:, bass.ds(col + j, 1)], ALU.is_equal, ALU.mult)
                                else:
                                    oh = dve.tensor_scalar(onehot[:, s % 2, j, :], iota1[:, :], key[:, j:j + 1],
                                                           None, ALU.is_equal)
                            oh.then_inc(onehot_ready, 1)
                            dve.wait_ge(scattered, step + 1)
                            dve.wait_ge(added, step)
                            dve.scalar_tensor_tensor(
                                acc[:, bass.ds(b0, 1), :].rearrange("p b f -> p (b f)"), bank_s[:, 0:F],
                                in_first[:, bass.ds(c, 1)],
                                acc[:, bass.ds(b0, 1), :].rearrange("p b f -> p (b f)"), ALU.mult, ALU.add)
                            dve.scalar_tensor_tensor(
                                acc[:, bass.ds(b0 + 1, 1), :].rearrange("p b f -> p (b f)"), bank_s[:, 0:F],
                                in_next[:, bass.ds(c, 1)],
                                acc[:, bass.ds(b0 + 1, 1), :].rearrange("p b f -> p (b f)"), ALU.mult, ALU.add
                            ).then_inc(added, 1)
                            dve.reg_add(steps, steps, 1)
                        dve.sem_inc(slot_freed, 1)

                dve.wait_ge(added, dve.snap(steps))
                normalise(l)

            link(dve.memset(acc[:, BLOCKS, :], 0.0))
            with dve.Fori(0, BLOCKS // 4) as g:
                dve.wait_ge(self_made, g + 2)
                dve.tensor_scalar(acc[:, bass.ds(g * 4, 4), :], psum[:, 0:4, 0:F], SI_SCALE / ALPHA, None,
                                  ALU.mult).then_inc(self_added, 1)

            def add_window(b0, c, before, fold, folded_sem, done):
                dve.tensor_reduce(folded[:, 0:MUL], bank_s[:, 0:MA].rearrange("p (o i) -> p o i", o=MUL), AX.X, ALU.add)
                dve.tensor_reduce(folded_q[:, :].rearrange("p (o m) -> p m o", m=3),
                                  bank_s[:, MQ:MSG].rearrange("p (m o i) -> p m o i", m=3, o=MUL), AX.X, ALU.add
                                  ).then_inc(fold, 1)
                dve.wait_ge(fold, before + 1)
                dve.tensor_tensor(folded[:, MUL:F], folded_q[:, :], bank_s[:, MA:MQ], ALU.add).then_inc(folded_sem, 1)
                dve.wait_ge(folded_sem, before + 1)
                for n, part_of in ((0, in_first), (1, in_next)):
                    to = acc[:, bass.ds(b0 + n, 1), :].rearrange("p b f -> p (b f)")
                    last = dve.scalar_tensor_tensor(to, folded[:, :], part_of[:, bass.ds(c, 1)], to, ALU.mult, ALU.add)
                last.then_inc(done, 1)

            def all_onehots(s):
                return dve.tensor_tensor(onehot[:, s % 2, :, :], iota1[:, :].unsqueeze(1).to_broadcast([P, TILES, P]),
                                         key[:, :].unsqueeze(2).to_broadcast([P, TILES, P]), ALU.is_equal)

            def onehots3(c, s):
                cols = bass.ds(c * TILES, TILES)
                dve.scalar_tensor_tensor(reached[:, :], dst_f[:, cols], base[:, bass.ds(c, 1)], dmod1[:, cols],
                                         ALU.is_ge, ALU.mult).then_inc(reach3_ready, 1)
                dve.tensor_scalar(window_end[:, :], base[:, bass.ds(c, 1)], float(P), None, ALU.add
                                  ).then_inc(window3_ready, 1)
                dve.wait_ge(reach3_ready, c + 1)
                dve.wait_ge(window3_ready, c + 1)
                dve.scalar_tensor_tensor(key[:, :], dst_f[:, cols], window_end[:, 0:1], reached[:, :],
                                         ALU.is_lt, ALU.mult).then_inc(key3_ready, 1)
                dve.wait_ge(key3_ready, c + 1)
                all_onehots(s).then_inc(onehot3_ready, 1)

            def messages(c, s, it):
                dve.wait_ge(rows_in[3][s], it * (16 * TILES) + 16 * TILES)
                dve.wait_ge(edges_in[s], it * 32 + 32)
                zs = z[:, s % 2]
                v = gathered[:, s, :, MUL:F].rearrange("p j (i m) -> p j i m", m=3)
                sh1 = sh[:, s, :, 1:4]
                dve.tensor_tensor(cprod[:, :, :, :], v, sh1.unsqueeze(2).to_broadcast([P, TILES, MUL, 3]), ALU.mult
                                  ).then_inc(cprod_ready, 1)
                dve.wait_ge(cprod_ready, c + 1)
                dve.tensor_reduce(zs[:, :, 0:MUL], cprod[:, :, :, :], AX.X, ALU.add).then_inc(c_ready, 1)
                dve.wait_ge(c_ready, c + 1)
                dve.wait_ge(z_scaled, c + 1)
                for g in range(GROUP):
                    tiles = slice(GROUP * g, GROUP * g + GROUP)
                    group = c * GROUP + g
                    w = pair[g % 2].rearrange("p (j n) -> p j n", n=WN)
                    over_o = lambda ap, n: ap.unsqueeze(2).to_broadcast([P, GROUP, MUL, n])
                    split = lambda ap, n: ap.rearrange("p j (o n) -> p j o n", n=n)
                    dve.wait_ge(w_made, c * GROUP + (g + 2 * GROUP + 1))
                    dve.wait_ge(msg_ready, group + 1)
                    dve.tensor_tensor(prod_a[:, :, :, :], split(w[:, :, 0:A_END], 2 * MUL),
                                      over_o(zs[:, tiles, 0:2 * MUL], 2 * MUL), ALU.mult)
                    dve.tensor_tensor(prod_q[:, :, :, :], split(w[:, :, A_END:Q_END], MUL),
                                      over_o(gathered[:, s, tiles, 0:MUL], MUL), ALU.mult)
                    for m in range(3):
                        last = dve.tensor_tensor(
                            prod_v[:, :, m], split(w[:, :, Q_END:WN], MUL),
                            over_o(zs[:, tiles, ZC + m:5 * MUL:3], MUL), ALU.mult)
                    last.then_inc(products, 1)
                    dve.wait_ge(products, group + 1)
                    dve.sem_inc(pair_free, 1)
                    to = msg[:, s % 2, tiles]
                    dve.tensor_reduce(q_sum[:, :, :], prod_q[:, :, :, :], AX.X, ALU.add).then_inc(q_ready, 1)
                    dve.tensor_tensor(split(to[:, :, 0:MA], MUL), prod_a[:, :, :, 0:MUL], prod_a[:, :, :, MUL:],
                                      ALU.add)
                    half_v = prod_v[:, :, :, :, :].rearrange("p j m o i -> p j (m o) i")
                    dve.tensor_tensor(split(to[:, :, MQ:MSG], 4), half_v[:, :, :, 0:4], half_v[:, :, :, 4:8], ALU.add)
                    dve.wait_ge(q_ready, group + 1)
                    dve.tensor_tensor(split(to[:, :, MA:MQ], 3),
                                      q_sum[:, :, :].unsqueeze(3).to_broadcast([P, GROUP, MUL, 3]),
                                      sh1[:, tiles].unsqueeze(2).to_broadcast([P, GROUP, MUL, 3]), ALU.mult
                                      ).then_inc(msg_ready, 1)
                dve.wait_ge(msg_ready, c * GROUP + (GROUP + 1))
                dve.sem_inc(z_free, 1)
                dve.sem_inc(slot_freed, 1)

            extras = dve.alloc_register("dve_extras")
            dve.reg_mov(extras, 0)
            extra_chunks = dve.alloc_register("dve_extra_chunks")
            dve.reg_mov(extra_chunks, 0)

            def add_chunk(c, s):
                first_block = dve.value_load(meta[0:1, 0, bass.ds(c, 1)], min_val=0, max_val=BLOCKS - 1)
                second_block = dve.value_load(meta[0:1, 2, bass.ds(c, 1)], min_val=1, max_val=BLOCKS)
                end_block = dve.value_load(meta[0:1, 1, bass.ds(c, 1)], min_val=1, max_val=BLOCKS)
                dve.wait_ge(scattered3, c + 1)
                add_window(first_block, c, c, folds, folded_ready, added3)
                with dve.If(second_block < end_block):
                    cols = bass.ds(c * TILES, TILES)
                    dve.tensor_copy(window[:, :], base[:, bass.ds(c, 1)]).then_inc(extra["window"], 1)
                    dve.reg_add(extra_chunks, extra_chunks, 1)
                    nth = dve.snap(extra_chunks)
                    with dve.Fori(second_block, end_block) as b0:
                        n = dve.snap(extras)
                        dve.wait_ge(extra["window"], nth)
                        dve.wait_ge(extra["moved"], n * 2 + 1)
                        dve.tensor_scalar(window[:, :], window[:, :], float(P), None, ALU.add
                                          ).then_inc(extra["moved"], 1)
                        dve.wait_ge(extra["moved"], n * 2 + 2)
                        dve.scalar_tensor_tensor(reached[:, :], dst_f[:, cols], window[:, 0:1], dmod1[:, cols],
                                                 ALU.is_ge, ALU.mult).then_inc(extra["reached"], 1)
                        dve.tensor_scalar(window_end[:, :], window[:, :], float(P), None, ALU.add
                                          ).then_inc(extra["moved"], 1)
                        dve.wait_ge(extra["reached"], n + 1)
                        dve.wait_ge(extra["moved"], n * 2 + 3)
                        dve.scalar_tensor_tensor(key[:, :], dst_f[:, cols], window_end[:, 0:1], reached[:, :],
                                                 ALU.is_lt, ALU.mult).then_inc(extra["key"], 1)
                        dve.wait_ge(extra["key"], n + 1)
                        all_onehots(s).then_inc(extra["onehot"], 1)
                        dve.wait_ge(extra["scattered"], n + 1)
                        add_window(b0, c, n, extra["fold"], extra["folded"], extra["added"])
                        dve.wait_ge(extra["added"], n + 1)
                        dve.reg_add(extras, extras, 1)

            onehots3(0, 0)
            messages(0, 0, 0)
            for s in range(1, SLOTS):
                onehots3(s, s)
                messages(s, s, 0)
                add_chunk(s - 1, s - 1)
            with dve.Fori(1, ROUNDS) as it:
                for s in range(SLOTS):
                    onehots3(it * SLOTS + s, s)
                    messages(it * SLOTS + s, s, it)
                    add_chunk(it * SLOTS + (s - 1), (s - 1) % SLOTS)
            add_chunk(CHUNKS - 1, SLOTS - 1)
            dve.wait_ge(added3, CHUNKS + 1)
            normalise(3)
    return nc


_INS = ["x", "src", "dst", "edge_attr_32", "edge_attr_4", "edge_type_64", "edge_weight", "L0_gnn_weight",
        "L3_gnn_W1", "L3_gnn_b1", "L3_gnn_W2", "L3_gnn_b2", "L3_gnn_si_w0", "L3_gnn_si_w1"]


def kernel(**inputs):
    import numpy as np
    import concourse.bacc as bacc
    from concourse.bass_utils import run_bass_kernel_spmd

    nc = bacc.Bacc("TRN2", target_bir_lowering=False, num_devices=1)
    arrays, args = {}, []
    for name in _INS:
        a = np.ascontiguousarray(inputs[name])
        arrays[f"in_{name}"] = a
        args.append(nc.dram_tensor(f"in_{name}", a.shape, mybir.dt.from_np(a.dtype), kind="ExternalInput").ap())
    args.append(nc.dram_tensor("out", arrays["in_x"].shape, F32, kind="ExternalOutput").ap())
    build(nc, *args)
    return run_bass_kernel_spmd(nc, [arrays], core_ids=[0]).results[0]["out"]
```

```python
from contextlib import ExitStack

import concourse.bass as bass
from concourse import mybir

P = 128
F = 32
TILES = 16
CHUNK = TILES * P
FIRST = 0
SLOTS = 4
GROUP = 4
MUL = 8
SPAN = 8
SPAN_COLS = SPAN * 64
SPAN_TILES = 4
HALF = 1024

ALU = mybir.AluOpType
ACT = mybir.ActivationFunctionType
F32 = mybir.dt.float32
I32 = mybir.dt.int32
BF16 = mybir.dt.bfloat16
F16 = mybir.dt.float16
AX = mybir.AxisListType
ALPHA = 0.25
C110 = 3.0 ** -0.5
SI_SCALE = MUL ** -0.5
HID = 64
WN = 4 * MUL * MUL
A_END = 2 * MUL * MUL
Q_END = 3 * MUL * MUL
MA = MUL * MUL
MQ = MA + 3 * MUL
MSG = MQ + 3 * MUL * 4
ZC = 2 * MUL
SETUP_MINMAX = 8
SETUP_COL = 10
SETUP_ROW = 11


def build(nc, x, src, dst, edge_attr_32, edge_attr_4, edge_type_64, edge_weight, L0_gnn_weight,
          L3_gnn_W1, L3_gnn_b1, L3_gnn_W2, L3_gnn_b2, L3_gnn_si_w0, L3_gnn_si_w1, out):
    NODES = x.shape[0]
    EDGES = src.shape[0]
    RELS = L0_gnn_weight.shape[0]
    BLOCKS = NODES // P
    CHUNKS = EDGES // CHUNK
    COLS = CHUNKS * TILES
    ROUNDS = CHUNKS // SLOTS
    KT = COLS // P
    SPANS = NODES // SPAN
    KS = SPANS // P
    PER_CHUNK = SPANS // (2 * CHUNKS)
    PER_BLOCK = P // SPAN
    assert PER_CHUNK * SLOTS == PER_BLOCK and BLOCKS * SPAN == SPAN_COLS
    SPAN_MM, SPAN_LIMITS, SPAN_FL = 1, 3 + 4 * KS, 4 + 4 * KS
    assert CHUNKS == P and BLOCKS % 4 == 0 and RELS * F == 2 * HALF

    with ExitStack() as ctx:
        def sb(name, shape, dt=F32):
            return ctx.enter_context(nc.sbuf_tensor(name, shape, dt))

        def sem(name):
            return ctx.enter_context(nc.semaphore(name))

        rel_table = nc.dram_tensor("rel_table", [NODES * RELS, F], F32).ap()
        counts = nc.dram_tensor("counts", [BLOCKS, P, BLOCKS * P], F16).ap()
        rows = [rel_table] + [nc.dram_tensor(f"x_rows_{n}", [NODES, F], F32).ap() for n in (1, 2, 3)]

        ARENA = 15616
        arena = sb("arena", [P, ARENA])
        taken = [0]

        def cut(columns):
            a = arena[:, taken[0]:taken[0] + columns]
            taken[0] += columns
            assert taken[0] <= ARENA, taken[0]
            return a

        src_i = sb("src_i", [P, COLS], I32)
        dst_i = sb("dst_i", [P, COLS], I32)
        key_i = sb("key_i", [P, COLS], I32)
        dst_f = sb("dst_f", [P, COLS])
        dmod_i = sb("dmod_i", [P, COLS], I32)
        dmod1 = sb("dmod1", [P, COLS])
        weight = sb("weight", [P, COLS])

        dst_min = sb("dst_min", [P, CHUNKS])
        dst_max = sb("dst_max", [P, CHUNKS])
        col_min = sb("col_min", [P, 2])
        row_min = sb("row_min", [1, 2, CHUNKS])
        row_i = sb("row_i", [1, 2, CHUNKS], I32)
        meta = sb("meta", [1, CHUNKS, 3], I32)
        base = sb("base", [P, CHUNKS])
        base_i = sb("base_i", [P, CHUNKS], I32)
        basemod = sb("basemod", [P, CHUNKS])
        in_first = sb("in_first", [P, CHUNKS])
        in_next = sb("in_next", [P, CHUNKS])

        iota_i = sb("iota_i", [P, P], I32)
        iota1 = sb("iota1", [P, P])
        part_i = sb("part_i", [P, 1], I32)
        part = sb("part", [P, 1])
        part1 = sb("part1", [P, 1])
        ident = sb("ident", [P, P])
        ones = sb("ones", [1, P])
        epsc = sb("epsc", [P, 1])

        rel_w = sb("rel_w", [P, RELS * F])
        group_x = sb("group_x", [P, P])
        group_xT = sb("group_xT", [P, P])
        table_out = sb("table_out", [P, 2, RELS * F])
        table_flat = table_out[:, :, :].rearrange("p a b -> p (a b)")

        idx = sb("idx", [P, SLOTS, TILES], I32)
        gathered = sb("gathered", [P, SLOTS, TILES, F])
        onehot = sb("onehot", [P, 2, TILES, P])
        window = sb("window", [P, 1])
        window_end = sb("window_end", [P, 1])
        reached = sb("reached", [P, TILES])
        key = sb("key", [P, TILES])

        w1 = sb("w1", [P, HID + 1])
        bias1 = sb("bias1", [HID + 1, 1])
        w2_raw = sb("w2_raw", [HID + 1, WN])
        w2 = sb("w2", [HID + 1, WN])
        w_self = sb("w_self", [P, F])
        taken[0] = 0
        edge_in = cut(SLOTS * TILES * F).rearrange("p (s j f) -> p s j f", s=SLOTS, f=F)
        sh = sb("sh", [P, SLOTS, TILES, 4])
        edge_T = cut(GROUP * P)
        hidden = cut(2 * GROUP * GROUP * P).rearrange("p (s q n) -> p s q n", s=2, q=GROUP)[0:HID + 1]
        z = cut(2 * TILES * 5 * MUL).rearrange("p (s j f) -> p s j f", s=2, j=TILES)
        cprod = sb("cprod", [P, TILES, MUL, 3])
        prod_a = cut(GROUP * A_END).rearrange("p (j o i) -> p j o i", j=GROUP, o=MUL)
        prod_q = cut(GROUP * MUL * MUL).rearrange("p (j o i) -> p j o i", j=GROUP, o=MUL)
        prod_v = cut(GROUP * 3 * MUL * MUL).rearrange("p (j m o i) -> p j m o i", j=GROUP, m=3, o=MUL)
        q_sum = sb("q_sum", [P, GROUP, MUL])
        msg = cut(2 * TILES * MSG).rearrange("p (s j f) -> p s j f", s=2, j=TILES)
        folded = sb("folded", [P, F])
        folded_q = sb("folded_q", [P, 3 * MUL])

        pair_T = dst_i[:, :].bitcast(F32)
        low_T = dmod_i[:, :].bitcast(F32)
        iota_span = sb("iota_span", [P, SPAN_COLS], F16)
        iota_low = iota_span[:, 0:P]
        span_base = sb("span_base", [P, SPANS])
        tile_mm = sb("tile_mm", [P, 2 * KT])
        tile_mmT = sb("tile_mmT", [2 * KT, P])
        limits = sb("limits", [P, 2, KS])
        limits_i = sb("limits_i", [P, KS], I32)
        first_last = sb("first_last", [P, 2, KS])
        first_lastT = sb("first_lastT", [2 * KS, P])
        span_stat = sb("span_stat", [1, 4])
        dense_ok = sb("dense_ok", [1, 1], I32)
        row_space = onehot[0:1, :, :, :].rearrange("p a b c -> p (a b c)")
        tile_row = row_space
        range_f = row_space[:, 0:2 * SPANS]
        firsts = rel_w[0:1, 0:SPANS].bitcast(I32)
        taken[0] = 0
        src_r = cut(COLS).bitcast(I32)
        dst_r = cut(COLS).bitcast(I32)
        high_r = cut(COLS).bitcast(I32)
        low_r = cut(COLS)
        pair_r = cut(COLS)
        tile_no = cut(COLS)
        tile_no_i = tile_no.bitcast(I32)
        tile_back = cut(COLS)
        masked = src_r.bitcast(F32)
        taken[0] = 0
        counts_out = cut(BLOCKS * P // 2).bitcast(F16)
        counts_in = [cut(BLOCKS * P // 2).bitcast(F16) for _ in range(2)]
        rest = arena[:, taken[0]:taken[0] + BLOCKS * F].rearrange("p (b f) -> p b f", f=F)
        oh_pair = [[cut(SPAN_COLS // 2).bitcast(BF16) for _ in range(SPAN_TILES)] for _ in range(2)]
        oh_low = [[cut(P // 2).bitcast(BF16) for _ in range(SPAN_TILES)] for _ in range(2)]
        x_parts = table_flat[:, 0:BLOCKS * 3 * F // 2].bitcast(BF16).rearrange("p (b k f) -> p b k f", b=BLOCKS, k=3)

        xn = sb("xn", [P, BLOCKS, F])
        acc = sb("acc", [P, BLOCKS + 2, F])
        cen = table_out[:, 0, :].rearrange("p (b f) -> p b f", f=F)
        sq = table_out[:, 1, :].rearrange("p (b f) -> p b f", f=F)
        st1 = sb("st1", [P, BLOCKS])
        st2 = sb("st2", [P, BLOCKS])
        st3 = sb("st3", [P, BLOCKS])

        psum = ctx.enter_context(nc.psum_tensor("psum", [P, 8, 512], F32))
        pair = [psum[:, 2 * k:2 * k + 2, :].rearrange("p a b -> p (a b)") for k in range(2)]
        bank_t = psum[:, 4, :]
        bank_h = [psum[:, 5, :], psum[:, 6, :]]
        bank_s = psum[:, 7, :]

        loaded = sem("loaded")
        x_loaded = sem("x_loaded")
        rel_loaded = sem("rel_loaded")
        iota_done = sem("iota_done")
        setup = sem("setup")
        ident_done = sem("ident_done")
        turned = sem("turned")
        keys_ready = sem("keys_ready")
        meta_ready = sem("meta_ready")
        x_staged = sem("x_staged")
        x_turned = sem("x_turned")
        xT_ready = sem("xT_ready")
        table_mm = sem("table_mm")
        evac_a = sem("evac_a")
        evac_v = sem("evac_v")
        table_stored = [sem("table_stored_0"), sem("table_stored_1")]
        rows_in = [[sem(f"rows_in_{l}_{s}") for s in range(SLOTS)] for l in range(4)]
        window_set = sem("window_set")
        window_moved = sem("window_moved")
        reached_ready = sem("reached_ready")
        key_ready = sem("key_ready")
        onehot_ready = sem("onehot_ready")
        scattered = sem("scattered")
        added = sem("added")
        slot_freed = sem("slot_freed")
        sq_done = sem("sq_done")
        std_done = sem("std_done")
        x_ready = sem("x_ready")
        rows_out = [sem(f"rows_out_{l}") for l in range(4)]
        idx_in = [sem(f"idx_in_{s}") for s in range(SLOTS)]
        tiles_in = sem("tiles_in")
        split_ready = sem("split_ready")
        tiles_turned = sem("tiles_turned")
        tiles_T = sem("tiles_T")
        spans = sem("spans")
        span_turn = sem("span_turn")
        span_rows = sem("span_rows")
        ranges_ready = sem("ranges_ready")
        pairs_ready = sem("pairs_ready")
        span_done = sem("span_done")
        span_out = sem("span_out")
        counts_stored = sem("counts_stored")
        counts_loaded = [sem("counts_loaded_0"), sem("counts_loaded_1")]
        parts_ready = sem("parts_ready")
        block_sums = sem("block_sums")
        block_taken = sem("block_taken")
        zeroed = sem("zeroed")
        w3_loaded = sem("w3_loaded")
        w3_ready = sem("w3_ready")
        self_made = sem("self_made")
        self_added = sem("self_added")
        edges_in = [sem(f"edges_in_{s}") for s in range(SLOTS)]
        edges_turned = sem("edges_turned")
        edge_T_ready = sem("edge_T_ready")
        hidden_made = sem("hidden_made")
        hidden_ready = sem("hidden_ready")
        z_scaled = sem("z_scaled")
        z_free = sem("z_free")
        w_made = sem("w_made")
        pair_free = sem("pair_free")
        cprod_ready = sem("cprod_ready")
        c_ready = sem("c_ready")
        products = sem("products")
        q_ready = sem("q_ready")
        folds = sem("folds")
        msg_ready = sem("msg_ready")
        onehot3_ready = sem("onehot3_ready")
        key3_ready = sem("key3_ready")
        reach3_ready = sem("reach3_ready")
        window3_ready = sem("window3_ready")
        scattered3 = sem("scattered3")
        folded_ready = sem("folded_ready")
        added3 = sem("added3")
        extra = {n: sem("extra_" + n) for n in ("window", "moved", "reached", "key", "onehot", "scattered",
                                                 "fold", "folded", "added")}

        edge_cols = lambda a: a.rearrange("(c p j) -> p c j", p=P, j=TILES)
        node_rows = lambda a: a.rearrange("(b p) f -> p b f", p=P)
        cols3 = lambda t: t[:, :].rearrange("p (c j) -> p c j", j=TILES)

        edge_rows = edge_attr_32.rearrange("(c p j) f -> c p (j f)", p=P, j=TILES)
        sh_rows = edge_attr_4.rearrange("(c p j) f -> c p (j f)", p=P, j=TILES)
        W3_LOADS = 16 * (4 * 5 + 3)

        def numbers_at(eng, ap, least, most):
            return nc.values_load_multi_w_load_instructions(
                ap, [eng.engine], min_val=least, max_val=most,
                skip_runtime_bounds_check_because="worked out on the chip within these bounds")[1]

        def blocks_of(eng, c):
            return numbers_at(eng, meta[0:1, bass.ds(c, 1), :].rearrange("a c k -> a (c k)"), 0, BLOCKS)

        def is_dense(eng):
            return numbers_at(eng, dense_ok[0:1, 0:1], 0, 1)[0]

        block = ctx.enter_context(nc.Block())

        @block.sync
        def _(sp):
            sp.dma_start(xn[:, :, :], node_rows(x)).then_inc(x_loaded, 16)
            for q in range(4):
                sp.dma_start(rel_w[F * q:F * q + F, :].rearrange("i (r o) -> i r o", o=F),
                             L0_gnn_weight.rearrange("r i o -> i r o")).then_inc(rel_loaded, 16)
            sp.dma_start(cols3(dst_i), edge_cols(dst)).then_inc(loaded, 16)
            sp.dma_start(cols3(src_i), edge_cols(src)).then_inc(loaded, 16)
            sp.dma_start(cols3(key_i), edge_cols(edge_type_64)).then_inc(loaded, 16)
            sp.dma_start(cols3(weight), edge_cols(edge_weight)).then_inc(loaded, 16)

            by_tile = lambda a: a.rearrange("(k q e) -> q k e", q=P, e=P)
            sp.dma_start(src_r.rearrange("q (k e) -> q k e", e=P), by_tile(src)).then_inc(tiles_in, 16)
            sp.dma_start(dst_r.rearrange("q (k e) -> q k e", e=P), by_tile(dst)).then_inc(tiles_in, 16)

            sp.wait_ge(zeroed, 1)
            for q in range(4):
                sp.dma_start(w1[F * q:F * q + F, 0:HID], L3_gnn_W1).then_inc(w3_loaded, 16)
                sp.dma_start(w_self[F * q:F * q + MUL, 0:MUL], L3_gnn_si_w0).then_inc(w3_loaded, 16)
                for m in range(3):
                    sp.dma_start(w_self[F * q + MUL + m:F * q + F:3, MUL + m:F:3], L3_gnn_si_w1, allow_slow_non_contiguous=True
                                 ).then_inc(w3_loaded, 16)
            sp.dma_start(bias1[0:HID, :], L3_gnn_b1.rearrange("(h a) -> h a", a=1)).then_inc(w3_loaded, 16)
            sp.dma_start(w2_raw[0:HID, :], L3_gnn_W2).then_inc(w3_loaded, 16)
            sp.dma_start(w2_raw[HID:HID + 1, :], L3_gnn_b2.rearrange("(a n) -> a n", a=1)).then_inc(w3_loaded, 16)

            table_rows = rel_table.rearrange("(b p r) o -> b p (r o)", p=P, r=RELS)
            with sp.Fori(0, BLOCKS // 2) as it:
                for h in range(2):
                    sp.wait_ge(evac_a, it * 2 + (h + 1))
                    sp.wait_ge(evac_v, it * 2 + (h + 1))
                    sp.dma_start(table_rows[bass.ds(it * 2 + h, 1), :, :].rearrange("b p c -> p (b c)"),
                                 table_out[:, h, :]).then_inc(table_stored[h], 16)

            sp.wait_ge(spans, SPAN_MM)
            sp.dma_start(tile_row.rearrange("p (k q) -> p k q", q=P), tile_mmT[:, :]).then_inc(span_rows, 16)

            def stage(l):
                numbers = key_i if l == 0 else src_i
                with sp.Fori(0, ROUNDS) as it:
                    for s in range(SLOTS):
                        c = it * SLOTS + s
                        sp.wait_ge(slot_freed, it * SLOTS + (l * CHUNKS + s + 1))
                        sp.dma_start(idx[:, s, :], numbers[:, bass.ds(it * (SLOTS * TILES) + s * TILES, TILES)]
                                     ).then_inc(idx_in[s], 16)
                        if l == 3:
                            sp.dma_start(edge_in[:, s, :, :].rearrange("p j f -> p (j f)"),
                                         edge_rows[bass.ds(c, 1), :, :].rearrange("c p k -> p (c k)")
                                         ).then_inc(edges_in[s], 16)
                            sp.dma_start(sh[:, s, :, :].rearrange("p j f -> p (j f)"),
                                         sh_rows[bass.ds(c, 1), :, :].rearrange("c p k -> p (c k)")
                                         ).then_inc(edges_in[s], 16)

            sp.wait_ge(keys_ready, 1)
            stage(0)
            stage(1)
            sp.wait_ge(ranges_ready, 1)
            dense = is_dense(sp)
            with sp.If(dense):
                sp.wait_ge(counts_stored, 16 * BLOCKS)
                for h in range(2):
                    sp.dma_start(counts_in[h], counts[h]).then_inc(counts_loaded[h], 16)
                with sp.Fori(1, BLOCKS // 2) as it:
                    for h in range(2):
                        sp.wait_ge(block_sums, it * 2 + (h - 1))
                        sp.dma_start(counts_in[h], counts[bass.ds(it * 2 + h, 1), :, :].rearrange("b p n -> p (b n)")
                                     ).then_inc(counts_loaded[h], 16)
            with sp.Else():
                stage(2)
            stage(3)

        @block.gpsimd
        def _(pool):
            pool.iota(iota_i[:, :], [[1, P]], base=1, channel_multiplier=0).then_inc(iota_done, 1)
            pool.iota(part_i[:, :], [[1, 1]], base=0, channel_multiplier=1).then_inc(iota_done, 1)
            pool.iota(tile_no_i, [[1, COLS]], base=1, channel_multiplier=0).then_inc(iota_done, 1)
            pool.iota(limits_i[:, :], [[P * SPAN, KS]], base=0, channel_multiplier=SPAN).then_inc(iota_done, 1)
            for s in table_stored:
                pool.wait_ge(s, 16 * (BLOCKS // 2))
            due = [pool.alloc_register(f"idx_due_{s}") for s in range(SLOTS)]
            for s in range(SLOTS):
                pool.reg_mov(due[s], 16)
            def gather(l):
                if l >= 1:
                    pool.wait_ge(rows_out[l - 1], 16)
                with pool.Fori(0, ROUNDS) as it:
                    for s in range(SLOTS):
                        pool.wait_ge(idx_in[s], pool.snap(due[s]))
                        pool.reg_add(due[s], due[s], 16)
                        for j in range(TILES):
                            pool.indirect_dma_start(
                                gathered[:, s, j, :], None, rows[l],
                                bass.IndirectOffsetOnAxis(ap=idx[:, s, j:j + 1], axis=0),
                            ).then_inc(rows_in[l][s], 16)

            gather(0)
            gather(1)
            dense = is_dense(pool)
            with pool.If(dense < 1):
                gather(2)
            gather(3)

        @block.scalar
        def _(act):
            def table_group(g):
                if g is not FIRST:
                    act.wait_ge(x_turned, g)
                act.copy(group_x[:, :], xn[:, bass.ds(g * 4, 4), :].rearrange("p b f -> p (b f)")
                         ).then_inc(x_staged, 1)
                act.wait_ge(x_turned, g + 1)
                if g is not FIRST:
                    act.wait_ge(table_mm, g * 8)
                act.copy(group_xT[:, :], bank_t[:, 0:P]).then_inc(xT_ready, 1)
                for q in range(4):
                    h = q % 2
                    act.wait_ge(table_mm, g * 8 + (2 * q + 1))
                    if g is not FIRST or q >= 2:
                        act.wait_ge(table_stored[h], g * 32 + 16 * (q // 2))
                    act.copy(table_out[:, h, 0:HALF], pair[0]).then_inc(evac_a, 1)

            act.wait_ge(x_loaded, 16)
            table_group(FIRST)
            with act.Fori(1, BLOCKS // 4) as g:
                table_group(g)

            def normalise(l):
                act.wait_ge(sq_done, 2 * l + 1)
                act.activation(sq[:, :, :], cen[:, :, :], ACT.Square).then_inc(sq_done, 1)
                act.wait_ge(std_done, 2 * l + 1)
                act.activation(st2[:, :], st1[:, :], ACT.Sqrt, bias=epsc[:, :], scale=1.0 / F).then_inc(std_done, 1)
                act.wait_ge(x_ready, l + 1)
                act.dma_start(node_rows(out if l == 3 else rows[l + 1]), xn[:, :, :]).then_inc(rows_out[l], 16)

            for n, to in ((0, pair_T), (1, low_T)):
                act.wait_ge(tiles_turned, n + 1)
                act.copy(to.rearrange("p (a b) -> p a b", b=512), psum[:, 4 * n:4 * n + 4, :]).then_inc(tiles_T, 1)
            act.wait_ge(spans, SPAN_FL)
            act.dma_start(range_f.rearrange("p (k q) -> p k q", q=P), first_lastT[:, :]).then_inc(span_rows, 16)

            for l in range(2):
                with act.Fori(0, ROUNDS) as it:
                    for s in range(SLOTS):
                        for i in range(PER_CHUNK):
                            n = s * PER_CHUNK + i
                            act.wait_ge(span_done, it * PER_BLOCK + (l * ROUNDS * PER_BLOCK + n + 3))
                            act.copy(counts_out.rearrange("p (h d) -> p d h", d=P)[:, SPAN * n:SPAN * n + SPAN, :],
                                         psum[:, i, :].rearrange("p (d h) -> p d h", d=SPAN)
                                         ).then_inc(span_out, 1)
                    act.wait_ge(span_out, it * PER_BLOCK + ((l * ROUNDS + 1) * PER_BLOCK + PER_CHUNK))
                    act.dma_start(counts[bass.ds(it + l * ROUNDS, 1), :, :].rearrange("b p n -> p (b n)"), counts_out
                                  ).then_inc(counts_stored, 16)
                    act.wait_ge(counts_stored, it * 16 + 16 * (l * ROUNDS + 1))
                normalise(l)
            normalise(2)

            with act.Fori(0, BLOCKS // 4) as g:
                act.wait_ge(x_turned, g + BLOCKS // 4)
                act.copy(group_x[:, :], xn[:, bass.ds(g * 4, 4), :].rearrange("p b f -> p (b f)")
                         ).then_inc(x_staged, 1)
                act.wait_ge(x_turned, g + (BLOCKS // 4 + 1))
                act.wait_ge(self_made, g + 1)
                act.copy(group_xT[:, :], bank_t[:, 0:P]).then_inc(xT_ready, 1)

            def hidden_units(c, s):
                act.wait_ge(edges_turned, c + 1)
                act.wait_ge(hidden_made, c * GROUP + 1)
                act.copy(edge_T[:, :], bank_t).then_inc(edge_T_ready, 1)
                for q in range(GROUP):
                    act.wait_ge(hidden_made, c * GROUP + (q + 2))
                    if q == 0:
                        act.wait_ge(w_made, c * GROUP + GROUP)
                    act.activation(hidden[:, s % 2, q, :], bank_h[q % 2][0:HID + 1, :], ACT.Relu,
                                   bias=bias1[:, :]).then_inc(hidden_ready, 1)

            def scale_rows(c, s, it):
                act.wait_ge(rows_in[3][s], it * (16 * TILES) + 16 * TILES)
                act.wait_ge(edges_in[s], it * 32 + 32)
                act.wait_ge(z_free, c + 1)
                for j in range(TILES):
                    a = act.activation(z[:, s % 2, j, MUL:], gathered[:, s, j, :], ACT.Copy,
                                       scale=sh[:, s, j, 0:1])
                a.then_inc(z_scaled, 1)

            act.wait_ge(w3_ready, 1)
            hidden_units(0, 0)
            with act.Fori(0, ROUNDS - 1) as it:
                for s in range(SLOTS):
                    scale_rows(it * SLOTS + s, s, it)
                    hidden_units(it * SLOTS + (s + 1), s + 1)
            for s in range(SLOTS):
                c = CHUNKS - SLOTS + s
                scale_rows(c, s, ROUNDS - 1)
                if c + 1 < CHUNKS:
                    hidden_units(c + 1, s + 1)
            normalise(3)
            act.wait_ge(rows_out[3], 16)

        @block.tensor
        def _(pe):
            pe.wait_ge(setup, SETUP_MINMAX)
            pe.wait_ge(ident_done, 1)
            pe.transpose(psum[:, 5, 0:P], dst_min[:, :], ident[:, :]).then_inc(turned, 1)
            pe.transpose(psum[:, 6, 0:P], dst_max[:, :], ident[:, :]).then_inc(turned, 1)
            pe.wait_ge(setup, SETUP_COL)
            pe.transpose(psum[0:1, 5, 0:P], col_min[:, 0:1], ident[:, :]).then_inc(turned, 1)
            pe.transpose(psum[0:1, 6, 0:P], col_min[:, 1:2], ident[:, :]).then_inc(turned, 1)
            pe.wait_ge(setup, SETUP_ROW)
            pe.matmul(psum[:, 5, 0:P], ones[:, :], row_min[0:1, 0, :], start=True, stop=True).then_inc(turned, 1)

            pe.wait_ge(rel_loaded, 64)
            def table_group(g):
                pe.wait_ge(x_staged, g + 1)
                if g is not FIRST:
                    pe.wait_ge(xT_ready, g)
                pe.transpose(bank_t[:, 0:P], group_x[:, :], ident[:, :]).then_inc(x_turned, 1)
                pe.wait_ge(xT_ready, g + 1)
                for q in range(4):
                    for k in range(2):
                        if g is not FIRST or q > 0:
                            pe.wait_ge((evac_a, evac_v)[k], g * 4 + q)
                        for n in range(2):
                            mm = pe.matmul(pair[k][:, 512 * n:512 * n + 512], group_xT[F * q:F * q + F, :],
                                           rel_w[F * q:F * q + F, HALF * k + 512 * n:HALF * k + 512 * n + 512],
                                           start=True, stop=True, tile_position=(F * q, 0))
                        mm.then_inc(table_mm, 1)

            table_group(FIRST)
            with pe.Fori(1, BLOCKS // 4) as g:
                table_group(g)

            pe.wait_ge(split_ready, 1)
            pe.wait_ge(evac_a, BLOCKS)
            pe.wait_ge(evac_v, BLOCKS)
            for n, what in ((0, pair_r), (1, low_r)):
                for k in range(KT):
                    t = pe.transpose(psum[:, 4 * n + k // 4, P * (k % 4):P * (k % 4) + P], what[:, P * k:P * k + P],
                                     ident[:, :])
                t.then_inc(tiles_turned, 1)
            pe.wait_ge(tiles_T, 2)
            pe.transpose(psum[0:2 * KT, 0, 0:P], tile_mm[:, :], ident[:, :]).then_inc(span_turn, 1)
            pe.wait_ge(span_rows, 16)
            for n in range(8):
                mm = pe.matmul(psum[:, n, :], ones[:, :], tile_row[:, 512 * n:512 * n + 512], start=True, stop=True)
            mm.then_inc(span_turn, 1)
            pe.wait_ge(spans, SPAN_LIMITS)
            pe.transpose(psum[0:2 * KS, 0, 0:P], first_last[:, :, :].rearrange("p a k -> p (a k)"), ident[:, :]
                         ).then_inc(span_turn, 1)

            def count_groups(n0):
                for i in range(PER_CHUNK):
                    pe.wait_ge(span_out, n0 + (i + 1))
                    pe.wait_ge(pairs_ready, n0 + (i + 1))
                    for k in range(SPAN_TILES):
                        mm = pe.matmul(psum[:, i, :], oh_low[i % 2][k], oh_pair[i % 2][k],
                                       start=(k == 0), stop=(k == SPAN_TILES - 1))
                    mm.then_inc(span_done, 1)

            pe.wait_ge(meta_ready, 1)
            pe.wait_ge(ranges_ready, 1)
            steps = pe.alloc_register("pe_steps")
            pe.reg_mov(steps, 1)

            def scatter_layer(l):
                with pe.Fori(0, ROUNDS) as it:
                    for s in range(SLOTS):
                        first_block, _, end_block = blocks_of(pe, it * SLOTS + s)
                        with pe.Fori(first_block, end_block):
                            step = pe.snap(steps)
                            pe.wait_ge(rows_in[l][s], it * (16 * TILES) + 16 * TILES)
                            pe.wait_ge(onehot_ready, step)
                            pe.wait_ge(added, step)
                            for j in range(TILES):
                                mm = pe.matmul(bank_s[:, 0:F], onehot[:, s % 2, j, :], gathered[:, s, j, :],
                                               start=(j == 0), stop=(j == TILES - 1))
                            mm.then_inc(scattered, 1)
                            pe.reg_add(steps, steps, 1)

                        if l < 2:
                            count_groups(it * PER_BLOCK + (l * ROUNDS * PER_BLOCK + s * PER_CHUNK))

            scatter_layer(0)
            scatter_layer(1)
            dense = is_dense(pe)
            with pe.If(dense):
                with pe.Fori(0, BLOCKS // 2) as it:
                    for h in range(2):
                        pe.wait_ge(parts_ready, 1)
                        pe.wait_ge(counts_loaded[h], it * 16 + 16)
                        pe.wait_ge(block_taken, it * 2 + (h + 1))
                        for k in range(BLOCKS):
                            mm = pe.matmul(psum[:, 4 + h, 0:3 * F], counts_in[h][:, P * k:P * k + P],
                                           x_parts[:, k, :, :].rearrange("p k f -> p (k f)"),
                                           start=(k == 0), stop=(k == BLOCKS - 1))
                        mm.then_inc(block_sums, 1)
            with pe.Else():
                scatter_layer(2)

            pe.wait_ge(w3_ready, 1)
            with pe.Fori(0, BLOCKS // 4) as g:
                pe.wait_ge(x_staged, g + (BLOCKS // 4 + 1))
                pe.wait_ge(xT_ready, g + BLOCKS // 4)
                pe.transpose(bank_t[:, 0:P], group_x[:, :], ident[:, :]).then_inc(x_turned, 1)
                pe.wait_ge(xT_ready, g + (BLOCKS // 4 + 1))
                pe.wait_ge(self_added, g + 1)
                for q in range(4):
                    mm = pe.matmul(psum[:, q, 0:F], group_xT[F * q:F * q + F, :], w_self[F * q:F * q + F, :],
                                   start=True, stop=True, tile_position=(F * q, 0))
                mm.then_inc(self_made, 1)
            pe.wait_ge(self_added, BLOCKS // 4 + 1)

            def turn_edges(c, s, it):
                pe.wait_ge(edges_in[s], it * 32 + 32)
                pe.wait_ge(edge_T_ready, c + 1)
                for g in range(GROUP):
                    t = pe.transpose(bank_t[:, P * g:P * g + P],
                                     edge_in[:, s, GROUP * g:GROUP * g + GROUP, :].rearrange("p j f -> p (j f)"),
                                     ident[:, :])
                t.then_inc(edges_turned, 1)

            def hidden_units(c):
                pe.wait_ge(edge_T_ready, c + 2)
                for q in range(GROUP):
                    pe.wait_ge(hidden_ready, c * GROUP + (q + 1))
                    pe.matmul(bank_h[q % 2][0:HID + 1, :], w1[F * q:F * q + F, :], edge_T[F * q:F * q + F, :],
                              start=True, stop=True, tile_position=(F * q, 0)).then_inc(hidden_made, 1)

            def edge_weights(c, s, g):
                if g == 0:
                    pe.wait_ge(hidden_ready, c * GROUP + (GROUP + 2))
                pe.wait_ge(pair_free, c * GROUP + (g + 1))
                for q in range(GROUP):
                    mm = pe.matmul(pair[g % 2][:, WN * q:WN * q + WN], hidden[:, s % 2, q, P * g:P * g + P], w2[:, :],
                                   start=True, stop=True)
                mm.then_inc(w_made, 1)

            def scatter(s, tiles):
                for j in tiles:
                    mm = pe.matmul(bank_s[:, 0:MSG], onehot[:, s % 2, j, :], msg[:, s % 2, j, :],
                                   start=(j == 0), stop=(j == TILES - 1))
                return mm

            def scatter_extra(c, s):
                _, second_block, end_block = blocks_of(pe, c)
                with pe.If(second_block < end_block):
                    with pe.Fori(second_block, end_block):
                        n = pe.snap(extras)
                        pe.wait_ge(extra["onehot"], n + 1)
                        scatter(s, range(TILES)).then_inc(extra["scattered"], 1)
                        pe.wait_ge(extra["added"], n + 1)
                        pe.reg_add(extras, extras, 1)

            extras = pe.alloc_register("pe_extras")
            pe.reg_mov(extras, 0)

            def chunk3(c, s, it, prev=True, following=True):
                if following:
                    turn_edges(c + 1, (s + 1) % SLOTS, it if s + 1 < SLOTS else it + 1)
                for g in range(GROUP):
                    edge_weights(c, s, g)
                    if g == 0 and following:
                        hidden_units(c + 1)
                    if prev:
                        if g == 0:
                            pe.wait_ge(onehot3_ready, c)
                            pe.wait_ge(msg_ready, c * GROUP + 1)
                            pe.wait_ge(added3, c)
                        mm = scatter((s - 1) % SLOTS, range(GROUP * g, GROUP * g + GROUP))
                if prev:
                    mm.then_inc(scattered3, 1)
                    scatter_extra(c - 1, (s - 1) % SLOTS)

            turn_edges(0, 0, 0)
            hidden_units(0)
            for s in range(SLOTS):
                chunk3(s, s, 0, prev=s > 0)
            with pe.Fori(1, ROUNDS - 1) as it:
                for s in range(SLOTS):
                    chunk3(it * SLOTS + s, s, it)
            for s in range(SLOTS):
                chunk3(CHUNKS - SLOTS + s, s, ROUNDS - 1, following=s + 1 < SLOTS)
            pe.wait_ge(onehot3_ready, CHUNKS)
            pe.wait_ge(msg_ready, CHUNKS * GROUP + 1)
            pe.wait_ge(added3, CHUNKS)
            scatter(SLOTS - 1, range(TILES)).then_inc(scattered3, 1)
            scatter_extra(CHUNKS - 1, SLOTS - 1)

        @block.vector
        def _(dve):
            chain = [0]

            def link(ins):
                chain[0] += 1
                ins.then_inc(setup, 1)
                dve.wait_ge(setup, chain[0])

            dve.memset(ones[:, :], 1.0)
            dve.memset(epsc[:, :], 1e-5)
            dve.memset(acc[:, :, :], 0.0)
            dve.memset(w1[:, :], 0.0)
            dve.memset(bias1[:, :], 1.0)
            dve.memset(w_self[:, :], 0.0).then_inc(zeroed, 1)
            for start, n in ((slot_freed, SLOTS), (z_free, 2), (pair_free, 2), (hidden_ready, 2), (hidden_made, 1),
                             (edge_T_ready, 1), (self_made, 1), (self_added, 1), (added3, 1), (w_made, 2 * GROUP),
                             (msg_ready, 1), (window_moved, 1), (key_ready, 1), (scattered, 1), (added, 1),
                             (extra["moved"], 1), (span_done, 2), (span_out, PER_CHUNK),
                             (block_taken, 2)):
                dve.sem_inc(start, n)
            dve.wait_ge(iota_done, 4)
            link(dve.tensor_copy(iota1[:, :], iota_i[:, :]))
            link(dve.tensor_copy(part[:, :], part_i[:, :]))
            link(dve.tensor_scalar(part1[:, :], part[:, :], 1.0, None, ALU.add))
            dve.tensor_scalar(ident[:, :], iota1[:, :], part1[:, 0:1], None, ALU.is_equal).then_inc(ident_done, 1)
            dve.wait_ge(loaded, 64)
            link(dve.tensor_copy(dst_f[:, :], dst_i[:, :]))
            link(dve.tensor_scalar(dmod_i[:, :], dst_i[:, :], P - 1, None, ALU.bitwise_and))
            link(dve.tensor_scalar(dmod1[:, :], dmod_i[:, :], 1.0, None, ALU.add))
            dve.scalar_tensor_tensor(key_i[:, :], src_i[:, :], float(RELS), key_i[:, :], ALU.mult,
                                     ALU.add).then_inc(keys_ready, 1)
            link(dve.tensor_reduce(dst_min[:, :], cols3(dst_f), AX.X, ALU.min))
            link(dve.tensor_reduce(dst_max[:, :], cols3(dst_f), AX.X, ALU.max))
            assert chain[0] == SETUP_MINMAX, chain[0]
            dve.wait_ge(turned, 2)
            link(dve.tensor_reduce(col_min[:, 0:1], psum[:, 5, 0:P], AX.X, ALU.min))
            link(dve.tensor_reduce(col_min[:, 1:2], psum[:, 6, 0:P], AX.X, ALU.max))
            assert chain[0] == SETUP_COL, chain[0]
            dve.wait_ge(turned, 4)
            link(dve.tensor_copy(row_min[0:1, 0, :], psum[0:1, 5, 0:P]))
            assert chain[0] == SETUP_ROW, chain[0]
            link(dve.tensor_tensor(row_min[0:1, 1, :], psum[0:1, 6, 0:P], row_min[0:1, 0, :], ALU.subtract))
            link(dve.tensor_copy(row_i[0:1, :, :], row_min[0:1, :, :]))
            link(dve.tensor_scalar(meta[0:1, :, 0:3:2].rearrange("a c k -> a k c"), row_i[0:1, :, :], 7, None,
                                   ALU.logical_shift_right))
            link(dve.tensor_scalar(meta[0:1, :, 1], meta[0:1, :, 0], 1.0, None, ALU.add))
            link(dve.scalar_tensor_tensor(meta[0:1, :, 2], meta[0:1, :, 2], 1.0, meta[0:1, :, 0], ALU.add, ALU.add))
            dve.wait_ge(turned, 5)
            link(dve.tensor_copy(base[:, :], psum[:, 5, 0:P]))
            link(dve.tensor_copy(base_i[:, :], base[:, :]))
            link(dve.tensor_scalar(base_i[:, :], base_i[:, :], P - 1, None, ALU.bitwise_and))
            link(dve.tensor_copy(basemod[:, :], base_i[:, :]))
            link(dve.tensor_scalar(in_first[:, :], basemod[:, :], part[:, 0:1], None, ALU.is_le))
            link(dve.tensor_scalar(in_next[:, :], basemod[:, :], part[:, 0:1], None, ALU.is_gt))
            dve.sem_inc(meta_ready, 1)

            dve.wait_ge(tiles_in, 32)
            link(dve.tensor_scalar(high_r, src_r, 7, None, ALU.logical_shift_right))
            link(dve.tensor_scalar(src_r, src_r, P - 1, None, ALU.bitwise_and))
            link(dve.tensor_copy(low_r, src_r))
            link(dve.scalar_tensor_tensor(pair_r, dst_r, float(BLOCKS), high_r, ALU.mult, ALU.add))
            link(dve.tensor_reduce(tile_mm[:, 0:KT], dst_r.rearrange("q (k e) -> q k e", e=P), AX.X, ALU.min))
            link(dve.tensor_reduce(tile_mm[:, KT:2 * KT], dst_r.rearrange("q (k e) -> q k e", e=P), AX.X, ALU.max))
            dve.sem_inc(split_ready, 1)
            link(dve.tensor_copy(tile_no, tile_no_i))
            link(dve.tensor_scalar(tile_back, tile_no, -1.0, COLS + 1.0, ALU.mult, ALU.add))
            link(dve.tensor_scalar(iota_span[:, :], tile_no[:, 0:SPAN_COLS], -1.0, None, ALU.add))
            link(dve.tensor_scalar(span_base[:, :], tile_no[:, 0:SPANS], -1.0, float(SPAN_COLS), ALU.add, ALU.mult))
            link(dve.tensor_copy(limits[:, 0, :], limits_i[:, :]))
            link(dve.tensor_scalar(limits[:, 1, :], limits[:, 0, :], SPAN - 1.0, None, ALU.add))

            dve.wait_ge(w3_loaded, W3_LOADS)
            raw = w2_raw[:, :].rearrange("h (k i o) -> h k o i", k=4, i=MUL)
            w2_a = w2[:, 0:A_END].rearrange("h (o k i) -> h k o i", o=MUL, k=2)
            oi = lambda ap: ap.rearrange("h (o i) -> h o i", o=MUL)
            dve.tensor_scalar(w2_a[:, 0], raw[:, 3], C110, None, ALU.mult)
            dve.tensor_copy(w2_a[:, 1], raw[:, 0])
            dve.tensor_copy(oi(w2[:, A_END:Q_END]), raw[:, 1])
            dve.tensor_copy(oi(w2[:, Q_END:WN]), raw[:, 2]).then_inc(w3_ready, 1)

            def normalise(l):
                if l >= 1:
                    dve.wait_ge(rows_out[l - 1], 16)
                if l == 3:
                    link(dve.scalar_tensor_tensor(xn[:, :, :], acc[:, 0:BLOCKS, :], ALPHA, xn[:, :, :],
                                                  ALU.mult, ALU.add))
                else:
                    link(dve.tensor_tensor(xn[:, :, :], xn[:, :, :], acc[:, 0:BLOCKS, :], ALU.add))
                link(dve.tensor_reduce(st1[:, :], xn[:, :, :], AX.X, ALU.add))
                link(dve.tensor_scalar(st1[:, :], st1[:, :], 1.0 / F, None, ALU.mult))
                dve.tensor_tensor(cen[:, :, :], xn[:, :, :], st1[:, :].unsqueeze(2).to_broadcast([P, BLOCKS, F]),
                                  ALU.subtract).then_inc(sq_done, 1)
                if l < 2:
                    link(dve.memset(acc[:, :, :], 0.0))
                dve.wait_ge(sq_done, 2 * l + 2)
                dve.tensor_reduce(st1[:, :], sq[:, :, :], AX.X, ALU.add).then_inc(std_done, 1)
                dve.wait_ge(std_done, 2 * l + 2)
                link(dve.reciprocal(st3[:, :], st2[:, :]))
                dve.tensor_tensor(xn[:, :, :], cen[:, :, :], st3[:, :].unsqueeze(2).to_broadcast([P, BLOCKS, F]),
                                  ALU.mult).then_inc(x_ready, 1)

            def table_group(g):
                for q in range(4):
                    h = q % 2
                    dve.wait_ge(table_mm, g * 8 + (2 * q + 2))
                    if g is not FIRST or q >= 2:
                        dve.wait_ge(table_stored[h], g * 32 + 16 * (q // 2))
                    dve.tensor_copy(table_out[:, h, HALF:2 * HALF], pair[1]).then_inc(evac_v, 1)

            table_group(FIRST)
            with dve.Fori(1, BLOCKS // 4) as g:
                table_group(g)

            count = [0]

            def span_link(ins):
                count[0] += 1
                ins.then_inc(spans, 1)
                dve.wait_ge(spans, count[0])

            dve.wait_ge(span_turn, 1)
            span_link(dve.tensor_copy(tile_mmT[:, :], psum[0:2 * KT, 0, 0:P]))
            dve.wait_ge(span_turn, 2)
            all_tiles = lambda n: psum[:, 4 * n:4 * n + 4, :].rearrange("p a b -> p (a b)")
            for k in range(KS):
                span_link(dve.scalar_tensor_tensor(masked, all_tiles(1), limits[:, 0, k:k + 1], tile_back,
                                                   ALU.is_ge, ALU.mult))
                span_link(dve.tensor_reduce(first_last[:, 0, k:k + 1], masked, AX.X, ALU.max))
                span_link(dve.scalar_tensor_tensor(masked, all_tiles(0), limits[:, 1, k:k + 1], tile_no,
                                                   ALU.is_le, ALU.mult))
                span_link(dve.tensor_reduce(first_last[:, 1, k:k + 1], masked, AX.X, ALU.max))
            span_link(dve.tensor_scalar(first_last[:, 0, :], first_last[:, 0, :], -1.0, float(COLS), ALU.mult, ALU.add))
            span_link(dve.tensor_scalar(first_last[:, 0, :], first_last[:, 0, :], float(COLS - SPAN_TILES), None,
                                        ALU.min))
            assert count[0] == SPAN_LIMITS
            dve.wait_ge(span_turn, 3)
            span_link(dve.tensor_copy(first_lastT[:, :], psum[0:2 * KS, 0, 0:P]))
            assert count[0] == SPAN_FL
            dve.wait_ge(span_rows, 32)
            length = row_space[:, 2 * SPANS:3 * SPANS]
            first_f, end_f = range_f[:, 0:SPANS], range_f[:, SPANS:2 * SPANS]
            span_link(dve.tensor_tensor(length, end_f, first_f, ALU.subtract))
            span_link(dve.tensor_reduce(span_stat[:, 0:1], length, AX.X, ALU.max))
            span_link(dve.tensor_scalar(span_stat[:, 1:2], span_stat[:, 0:1], float(SPAN_TILES), None, ALU.is_le))
            span_link(dve.tensor_copy(dense_ok[:, :], span_stat[:, 1:2]))
            span_link(dve.tensor_copy(firsts, first_f))
            dve.sem_inc(ranges_ready, 1)

            def count_groups(n0):
                first = numbers_at(dve, firsts[:, bass.ds(n0, PER_CHUNK)], 0, COLS - SPAN_TILES)
                for i in range(PER_CHUNK):
                    b = i % 2
                    dve.wait_ge(span_done, n0 + (i + 1))
                    for k in range(SPAN_TILES):
                        t = bass.ds(first[i] + k, 1)
                        dve.tensor_scalar(oh_low[b][k], iota_low, low_T[:, t], None, ALU.is_equal)
                        last = dve.tensor_scalar(oh_pair[b][k], iota_span[:, :], span_base[:, bass.ds(n0 + i, 1)],
                                                 pair_T[:, t], ALU.add, ALU.is_equal)
                    last.then_inc(pairs_ready, 1)

            steps = dve.alloc_register("dve_steps")
            dve.reg_mov(steps, 1)

            def scatter_layer(l):
                with dve.Fori(0, ROUNDS) as it:
                    for s in range(SLOTS):
                        c = it * SLOTS + s
                        col = it * (SLOTS * TILES) + s * TILES
                        first_block, _, end_block = blocks_of(dve, c)
                        chunk = it * SLOTS + (l * CHUNKS + s)
                        dve.wait_ge(window_moved, dve.snap(steps))
                        dve.tensor_copy(window[:, :], base[:, bass.ds(c, 1)]).then_inc(window_set, 1)
                        with dve.Fori(first_block, end_block) as b0:
                            step = dve.snap(steps)
                            dve.wait_ge(window_set, chunk + 1)
                            dve.wait_ge(window_moved, step)
                            dve.wait_ge(key_ready, step)
                            dve.scalar_tensor_tensor(reached[:, :], dst_f[:, bass.ds(col, TILES)], window[:, 0:1],
                                                     dmod1[:, bass.ds(col, TILES)], ALU.is_ge, ALU.mult
                                                     ).then_inc(reached_ready, 1)
                            dve.wait_ge(reached_ready, step)
                            dve.tensor_scalar(window[:, :], window[:, :], float(P), None, ALU.add
                                              ).then_inc(window_moved, 1)
                            dve.wait_ge(window_moved, step + 1)
                            dve.scalar_tensor_tensor(key[:, :], dst_f[:, bass.ds(col, TILES)], window[:, 0:1],
                                                     reached[:, :], ALU.is_lt, ALU.mult).then_inc(key_ready, 1)
                            dve.wait_ge(key_ready, step + 1)
                            dve.wait_ge(scattered, step)
                            for j in range(TILES):
                                if l == 1:
                                    oh = dve.tensor_scalar(onehot[:, s % 2, j, :], iota1[:, :], key[:, j:j + 1],
                                                           weight[:, bass.ds(col + j, 1)], ALU.is_equal, ALU.mult)
                                else:
                                    oh = dve.tensor_scalar(onehot[:, s % 2, j, :], iota1[:, :], key[:, j:j + 1],
                                                           None, ALU.is_equal)
                            oh.then_inc(onehot_ready, 1)
                            dve.wait_ge(scattered, step + 1)
                            dve.wait_ge(added, step)
                            dve.scalar_tensor_tensor(
                                acc[:, bass.ds(b0, 1), :].rearrange("p b f -> p (b f)"), bank_s[:, 0:F],
                                in_first[:, bass.ds(c, 1)],
                                acc[:, bass.ds(b0, 1), :].rearrange("p b f -> p (b f)"), ALU.mult, ALU.add)
                            dve.scalar_tensor_tensor(
                                acc[:, bass.ds(b0 + 1, 1), :].rearrange("p b f -> p (b f)"), bank_s[:, 0:F],
                                in_next[:, bass.ds(c, 1)],
                                acc[:, bass.ds(b0 + 1, 1), :].rearrange("p b f -> p (b f)"), ALU.mult, ALU.add
                            ).then_inc(added, 1)
                            dve.reg_add(steps, steps, 1)
                        dve.sem_inc(slot_freed, 1)

                        if l < 2:
                            count_groups(it * PER_BLOCK + (l * ROUNDS * PER_BLOCK + s * PER_CHUNK))
                dve.wait_ge(added, dve.snap(steps))

            scatter_layer(0)
            normalise(0)
            scatter_layer(1)
            normalise(1)
            dense = is_dense(dve)
            with dve.If(dense):
                dve.wait_ge(x_ready, 2)
                link(dve.tensor_copy(x_parts[:, :, 0, :], xn[:, :, :]))
                link(dve.tensor_tensor(rest, xn[:, :, :], x_parts[:, :, 0, :], ALU.subtract))
                link(dve.tensor_copy(x_parts[:, :, 1, :], rest))
                link(dve.tensor_tensor(rest, rest, x_parts[:, :, 1, :], ALU.subtract))
                dve.tensor_copy(x_parts[:, :, 2, :], rest).then_inc(parts_ready, 1)
                with dve.Fori(0, BLOCKS // 2) as it:
                    for h in range(2):
                        dve.wait_ge(block_sums, it * 2 + (h + 1))
                        dve.tensor_reduce(acc[:, bass.ds(it * 2 + h, 1), :].rearrange("p b f -> p (b f)"),
                                          psum[:, 4 + h, 0:3 * F].rearrange("p (k f) -> p f k", k=3), AX.X, ALU.add
                                          ).then_inc(block_taken, 1)
                dve.wait_ge(block_taken, BLOCKS + 2)
                dve.sem_inc(slot_freed, CHUNKS)
            with dve.Else():
                scatter_layer(2)
                dve.sem_inc(setup, 4)
            normalise(2)

            link(dve.memset(acc[:, BLOCKS:, :], 0.0))
            with dve.Fori(0, BLOCKS // 4) as g:
                dve.wait_ge(self_made, g + 2)
                dve.tensor_scalar(acc[:, bass.ds(g * 4, 4), :], psum[:, 0:4, 0:F], SI_SCALE / ALPHA, None,
                                  ALU.mult).then_inc(self_added, 1)

            def add_window(b0, c, before, fold, folded_sem, done):
                dve.tensor_reduce(folded[:, 0:MUL], bank_s[:, 0:MA].rearrange("p (o i) -> p o i", o=MUL), AX.X, ALU.add)
                dve.tensor_reduce(folded_q[:, :].rearrange("p (o m) -> p m o", m=3),
                                  bank_s[:, MQ:MSG].rearrange("p (m o i) -> p m o i", m=3, o=MUL), AX.X, ALU.add
                                  ).then_inc(fold, 1)
                dve.wait_ge(fold, before + 1)
                dve.tensor_tensor(folded[:, MUL:F], folded_q[:, :], bank_s[:, MA:MQ], ALU.add).then_inc(folded_sem, 1)
                dve.wait_ge(folded_sem, before + 1)
                for n, part_of in ((0, in_first), (1, in_next)):
                    to = acc[:, bass.ds(b0 + n, 1), :].rearrange("p b f -> p (b f)")
                    last = dve.scalar_tensor_tensor(to, folded[:, :], part_of[:, bass.ds(c, 1)], to, ALU.mult, ALU.add)
                last.then_inc(done, 1)

            def all_onehots(s):
                return dve.tensor_tensor(onehot[:, s % 2, :, :], iota1[:, :].unsqueeze(1).to_broadcast([P, TILES, P]),
                                         key[:, :].unsqueeze(2).to_broadcast([P, TILES, P]), ALU.is_equal)

            def onehots3(c, s):
                cols = bass.ds(c * TILES, TILES)
                dve.scalar_tensor_tensor(reached[:, :], dst_f[:, cols], base[:, bass.ds(c, 1)], dmod1[:, cols],
                                         ALU.is_ge, ALU.mult).then_inc(reach3_ready, 1)
                dve.tensor_scalar(window_end[:, :], base[:, bass.ds(c, 1)], float(P), None, ALU.add
                                  ).then_inc(window3_ready, 1)
                dve.wait_ge(reach3_ready, c + 1)
                dve.wait_ge(window3_ready, c + 1)
                dve.scalar_tensor_tensor(key[:, :], dst_f[:, cols], window_end[:, 0:1], reached[:, :],
                                         ALU.is_lt, ALU.mult).then_inc(key3_ready, 1)
                dve.wait_ge(key3_ready, c + 1)
                all_onehots(s).then_inc(onehot3_ready, 1)

            def messages(c, s, it):
                dve.wait_ge(rows_in[3][s], it * (16 * TILES) + 16 * TILES)
                dve.wait_ge(edges_in[s], it * 32 + 32)
                zs = z[:, s % 2]
                v = gathered[:, s, :, MUL:F].rearrange("p j (i m) -> p j i m", m=3)
                sh1 = sh[:, s, :, 1:4]
                dve.tensor_tensor(cprod[:, :, :, :], v, sh1.unsqueeze(2).to_broadcast([P, TILES, MUL, 3]), ALU.mult
                                  ).then_inc(cprod_ready, 1)
                dve.wait_ge(cprod_ready, c + 1)
                dve.tensor_reduce(zs[:, :, 0:MUL], cprod[:, :, :, :], AX.X, ALU.add).then_inc(c_ready, 1)
                dve.wait_ge(c_ready, c + 1)
                dve.wait_ge(z_scaled, c + 1)
                for g in range(GROUP):
                    tiles = slice(GROUP * g, GROUP * g + GROUP)
                    group = c * GROUP + g
                    w = pair[g % 2].rearrange("p (j n) -> p j n", n=WN)
                    over_o = lambda ap, n: ap.unsqueeze(2).to_broadcast([P, GROUP, MUL, n])
                    split = lambda ap, n: ap.rearrange("p j (o n) -> p j o n", n=n)
                    dve.wait_ge(w_made, c * GROUP + (g + 2 * GROUP + 1))
                    dve.wait_ge(msg_ready, group + 1)
                    dve.tensor_tensor(prod_a[:, :, :, :], split(w[:, :, 0:A_END], 2 * MUL),
                                      over_o(zs[:, tiles, 0:2 * MUL], 2 * MUL), ALU.mult)
                    dve.tensor_tensor(prod_q[:, :, :, :], split(w[:, :, A_END:Q_END], MUL),
                                      over_o(gathered[:, s, tiles, 0:MUL], MUL), ALU.mult)
                    for m in range(3):
                        last = dve.tensor_tensor(
                            prod_v[:, :, m], split(w[:, :, Q_END:WN], MUL),
                            over_o(zs[:, tiles, ZC + m:5 * MUL:3], MUL), ALU.mult)
                    last.then_inc(products, 1)
                    dve.wait_ge(products, group + 1)
                    dve.sem_inc(pair_free, 1)
                    to = msg[:, s % 2, tiles]
                    dve.tensor_reduce(q_sum[:, :, :], prod_q[:, :, :, :], AX.X, ALU.add).then_inc(q_ready, 1)
                    dve.tensor_tensor(split(to[:, :, 0:MA], MUL), prod_a[:, :, :, 0:MUL], prod_a[:, :, :, MUL:],
                                      ALU.add)
                    half_v = prod_v[:, :, :, :, :].rearrange("p j m o i -> p j (m o) i")
                    dve.tensor_tensor(split(to[:, :, MQ:MSG], 4), half_v[:, :, :, 0:4], half_v[:, :, :, 4:8], ALU.add)
                    dve.wait_ge(q_ready, group + 1)
                    dve.tensor_tensor(split(to[:, :, MA:MQ], 3),
                                      q_sum[:, :, :].unsqueeze(3).to_broadcast([P, GROUP, MUL, 3]),
                                      sh1[:, tiles].unsqueeze(2).to_broadcast([P, GROUP, MUL, 3]), ALU.mult
                                      ).then_inc(msg_ready, 1)
                dve.wait_ge(msg_ready, c * GROUP + (GROUP + 1))
                dve.sem_inc(z_free, 1)
                dve.sem_inc(slot_freed, 1)

            extras = dve.alloc_register("dve_extras")
            dve.reg_mov(extras, 0)
            extra_chunks = dve.alloc_register("dve_extra_chunks")
            dve.reg_mov(extra_chunks, 0)

            def add_chunk(c, s):
                first_block, second_block, end_block = blocks_of(dve, c)
                dve.wait_ge(scattered3, c + 1)
                add_window(first_block, c, c, folds, folded_ready, added3)
                with dve.If(second_block < end_block):
                    cols = bass.ds(c * TILES, TILES)
                    dve.tensor_copy(window[:, :], base[:, bass.ds(c, 1)]).then_inc(extra["window"], 1)
                    dve.reg_add(extra_chunks, extra_chunks, 1)
                    nth = dve.snap(extra_chunks)
                    with dve.Fori(second_block, end_block) as b0:
                        n = dve.snap(extras)
                        dve.wait_ge(extra["window"], nth)
                        dve.wait_ge(extra["moved"], n * 2 + 1)
                        dve.tensor_scalar(window[:, :], window[:, :], float(P), None, ALU.add
                                          ).then_inc(extra["moved"], 1)
                        dve.wait_ge(extra["moved"], n * 2 + 2)
                        dve.scalar_tensor_tensor(reached[:, :], dst_f[:, cols], window[:, 0:1], dmod1[:, cols],
                                                 ALU.is_ge, ALU.mult).then_inc(extra["reached"], 1)
                        dve.tensor_scalar(window_end[:, :], window[:, :], float(P), None, ALU.add
                                          ).then_inc(extra["moved"], 1)
                        dve.wait_ge(extra["reached"], n + 1)
                        dve.wait_ge(extra["moved"], n * 2 + 3)
                        dve.scalar_tensor_tensor(key[:, :], dst_f[:, cols], window_end[:, 0:1], reached[:, :],
                                                 ALU.is_lt, ALU.mult).then_inc(extra["key"], 1)
                        dve.wait_ge(extra["key"], n + 1)
                        all_onehots(s).then_inc(extra["onehot"], 1)
                        dve.wait_ge(extra["scattered"], n + 1)
                        add_window(b0, c, n, extra["fold"], extra["folded"], extra["added"])
                        dve.wait_ge(extra["added"], n + 1)
                        dve.reg_add(extras, extras, 1)

            onehots3(0, 0)
            messages(0, 0, 0)
            for s in range(1, SLOTS):
                onehots3(s, s)
                messages(s, s, 0)
                add_chunk(s - 1, s - 1)
            with dve.Fori(1, ROUNDS) as it:
                for s in range(SLOTS):
                    onehots3(it * SLOTS + s, s)
                    messages(it * SLOTS + s, s, it)
                    add_chunk(it * SLOTS + (s - 1), (s - 1) % SLOTS)
            add_chunk(CHUNKS - 1, SLOTS - 1)
            dve.wait_ge(added3, CHUNKS + 1)
            normalise(3)
    return nc


_INS = ["x", "src", "dst", "edge_attr_32", "edge_attr_4", "edge_type_64", "edge_weight", "L0_gnn_weight",
        "L3_gnn_W1", "L3_gnn_b1", "L3_gnn_W2", "L3_gnn_b2", "L3_gnn_si_w0", "L3_gnn_si_w1"]


def kernel(**inputs):
    import numpy as np
    import concourse.bacc as bacc
    from concourse.bass_utils import run_bass_kernel_spmd

    nc = bacc.Bacc("TRN2", target_bir_lowering=False, num_devices=1)
    arrays, args = {}, []
    for name in _INS:
        a = np.ascontiguousarray(inputs[name])
        arrays[f"in_{name}"] = a
        args.append(nc.dram_tensor(f"in_{name}", a.shape, mybir.dt.from_np(a.dtype), kind="ExternalInput").ap())
    args.append(nc.dram_tensor("out", arrays["in_x"].shape, F32, kind="ExternalOutput").ap())
    build(nc, *args)
    return run_bass_kernel_spmd(nc, [arrays], core_ids=[0]).results[0]["out"]
```

```python
from contextlib import ExitStack

import concourse.bass as bass
from concourse import mybir

P = 128
F = 32
TILES = 16
CHUNK = TILES * P
FIRST = 0
SLOTS = 4
GROUP = 4
MUL = 8
SPAN = 8
SPAN_COLS = SPAN * 64
SPAN_TILES = 4
HALF = 1024

ALU = mybir.AluOpType
ACT = mybir.ActivationFunctionType
F32 = mybir.dt.float32
I32 = mybir.dt.int32
BF16 = mybir.dt.bfloat16
F16 = mybir.dt.float16
AX = mybir.AxisListType
ALPHA = 0.25
C110 = 3.0 ** -0.5
SI_SCALE = MUL ** -0.5
HID = 64
WN = 4 * MUL * MUL
A_END = 2 * MUL * MUL
Q_END = 3 * MUL * MUL
MA = MUL * MUL
MQ = MA + 3 * MUL
MSG = MQ + 3 * MUL * 4
ZC = 2 * MUL
SETUP_REL = 6
SETUP_MINMAX = SETUP_REL + 8
SETUP_COL = SETUP_REL + 10
SETUP_ROW = SETUP_REL + 11
SPLIT_X = 6


def build(nc, x, src, dst, edge_attr_32, edge_attr_4, edge_type_64, edge_weight, L0_gnn_weight,
          L3_gnn_W1, L3_gnn_b1, L3_gnn_W2, L3_gnn_b2, L3_gnn_si_w0, L3_gnn_si_w1, out):
    NODES = x.shape[0]
    EDGES = src.shape[0]
    RELS = L0_gnn_weight.shape[0]
    BLOCKS = NODES // P
    CHUNKS = EDGES // CHUNK
    COLS = CHUNKS * TILES
    ROUNDS = CHUNKS // SLOTS
    KT = COLS // P
    SPANS = NODES // SPAN
    KS = SPANS // P
    PER_CHUNK = SPANS // (2 * CHUNKS)
    PER_BLOCK = P // SPAN
    assert PER_CHUNK * SLOTS == PER_BLOCK and BLOCKS * SPAN == SPAN_COLS
    SPAN_MM, SPAN_LIMITS, SPAN_FL = 1, 3 + 4 * KS, 4 + 4 * KS
    assert CHUNKS == P and BLOCKS % 4 == 0 and RELS * F == 2 * HALF

    with ExitStack() as ctx:
        def sb(name, shape, dt=F32):
            return ctx.enter_context(nc.sbuf_tensor(name, shape, dt))

        def sem(name):
            return ctx.enter_context(nc.semaphore(name))

        rel_table = nc.dram_tensor("rel_table", [NODES * RELS, F], F32).ap()
        counts = nc.dram_tensor("counts", [BLOCKS, P, BLOCKS * P], F16).ap()
        rows = [rel_table] + [nc.dram_tensor(f"x_rows_{n}", [NODES, F], F32).ap() for n in (1, 2, 3)]

        ARENA = 15616
        arena = sb("arena", [P, ARENA])
        taken = [0]

        def cut(columns):
            a = arena[:, taken[0]:taken[0] + columns]
            taken[0] += columns
            assert taken[0] <= ARENA, taken[0]
            return a

        src_i = sb("src_i", [P, COLS], I32)
        dst_i = sb("dst_i", [P, COLS], I32)
        key_i = sb("key_i", [P, COLS], I32)
        dst_f = sb("dst_f", [P, COLS])
        dmod_i = sb("dmod_i", [P, COLS], I32)
        key_all = sb("key_all", [P, COLS])
        weight = sb("weight", [P, COLS])

        dst_min = sb("dst_min", [P, CHUNKS])
        dst_max = sb("dst_max", [P, CHUNKS])
        col_min = sb("col_min", [P, 2])
        row_min = sb("row_min", [1, 2, CHUNKS])
        row_i = sb("row_i", [1, 2, CHUNKS], I32)
        meta = sb("meta", [1, CHUNKS, 3], I32)
        base = sb("base", [P, CHUNKS])
        base_end = sb("base_end", [P, CHUNKS])
        base_i = sb("base_i", [P, CHUNKS], I32)
        basemod = sb("basemod", [P, CHUNKS])
        in_first = sb("in_first", [P, CHUNKS])
        in_next = sb("in_next", [P, CHUNKS])

        iota_i = sb("iota_i", [P, P], I32)
        iota1 = sb("iota1", [P, P])
        part_i = sb("part_i", [P, 1], I32)
        part = sb("part", [P, 1])
        part1 = sb("part1", [P, 1])
        ident = sb("ident", [P, P])
        ones = sb("ones", [1, P])
        epsc = sb("epsc", [P, 1])
        one_col = sb("one_col", [P, 1])

        rel_w = sb("rel_w", [P, RELS * F])
        group_xT = sb("group_xT", [P, P])
        group_parts = sb("group_parts", [P, 4 * P])
        group_x = group_parts[:, 0:P]
        group_parts_T = sb("group_parts_T", [P, 4 * P], BF16)
        table_out = sb("table_out", [P, 2, RELS * F])
        table_flat = table_out[:, :, :].rearrange("p a b -> p (a b)")

        idx = sb("idx", [P, SLOTS, TILES], I32)
        gathered = sb("gathered", [P, SLOTS, TILES, F])
        onehot = sb("onehot", [P, 2, TILES, P])
        window = sb("window", [P, 1])
        window_end = sb("window_end", [P, 1])
        mod_i = sb("mod_i", [P, TILES], I32)
        mod1 = sb("mod1", [P, TILES])
        mod_out = sb("mod_out", [P, TILES], I32)
        reached = sb("reached", [P, TILES])
        key = sb("key", [P, TILES])

        node_parts = onehot[:, :, :, :].rearrange("p a b c -> p (a b c)").bitcast(BF16).rearrange(
            "p (b k f) -> p b k f", k=4, f=F)
        PASS_ROWS = (P, 3 * F, 3 * F)
        slots_flat = gathered[:, :, :, :].rearrange("p a b c -> p (a b c)").bitcast(BF16)

        w1 = sb("w1", [P, HID + 1])
        bias1 = sb("bias1", [HID + 1, 1])
        w2_raw = sb("w2_raw", [HID + 1, WN])
        w2 = sb("w2", [HID + 1, WN])
        w_self = sb("w_self", [P, F])
        taken[0] = 0
        edge_in = cut(SLOTS * TILES * F).rearrange("p (s j f) -> p s j f", s=SLOTS, f=F)
        sh = sb("sh", [P, SLOTS, TILES, 4])
        edge_T = cut(GROUP * P)
        hidden = cut(2 * GROUP * GROUP * P).rearrange("p (s q n) -> p s q n", s=2, q=GROUP)[0:HID + 1]
        z = cut(2 * TILES * 5 * MUL).rearrange("p (s j f) -> p s j f", s=2, j=TILES)
        cprod = sb("cprod", [P, TILES, MUL, 3])
        prod_a = cut(GROUP * A_END).rearrange("p (j o i) -> p j o i", j=GROUP, o=MUL)
        prod_q = cut(GROUP * MUL * MUL).rearrange("p (j o i) -> p j o i", j=GROUP, o=MUL)
        prod_v = cut(GROUP * 3 * MUL * MUL).rearrange("p (j m o i) -> p j m o i", j=GROUP, m=3, o=MUL)
        q_sum = sb("q_sum", [P, GROUP, MUL])
        msg = cut(2 * TILES * MSG).rearrange("p (s j f) -> p s j f", s=2, j=TILES)
        folded = sb("folded", [P, F])
        folded_q = sb("folded_q", [P, 3 * MUL])

        pair_T = dst_i[:, :].bitcast(F32)
        low_T = dmod_i[:, :].bitcast(F32)
        iota_span = sb("iota_span", [P, SPAN_COLS], F16)
        iota_low = iota_span[:, 0:P]
        span_base = sb("span_base", [P, SPANS])
        tile_mm = sb("tile_mm", [P, 2 * KT])
        tile_mmT = sb("tile_mmT", [2 * KT, P])
        limits = sb("limits", [P, 2, KS])
        limits_i = sb("limits_i", [P, KS], I32)
        first_last = sb("first_last", [P, 2, KS])
        first_lastT = sb("first_lastT", [2 * KS, P])
        span_stat = sb("span_stat", [1, 4])
        dense_ok = sb("dense_ok", [1, 1], I32)
        row_space = onehot[0:1, :, :, :].rearrange("p a b c -> p (a b c)")
        tile_row = row_space
        range_f = row_space[:, 0:2 * SPANS]
        firsts = rel_w[0:1, 0:SPANS].bitcast(I32)
        taken[0] = 0
        src_r = cut(COLS).bitcast(I32)
        dst_r = cut(COLS).bitcast(I32)
        high_r = cut(COLS).bitcast(I32)
        low_r = cut(COLS)
        pair_r = cut(COLS)
        tile_no = cut(COLS)
        tile_no_i = tile_no.bitcast(I32)
        tile_back = cut(COLS)
        masked = src_r.bitcast(F32)
        taken[0] = 0
        counts_out = cut(BLOCKS * P // 2).bitcast(F16)
        counts_in = [cut(BLOCKS * P // 2).bitcast(F16) for _ in range(2)]
        rest = arena[:, taken[0]:taken[0] + BLOCKS * F].rearrange("p (b f) -> p b f", f=F)
        oh_pair = [[cut(SPAN_COLS // 2).bitcast(BF16) for _ in range(SPAN_TILES)] for _ in range(2)]
        oh_low = [[cut(P // 2).bitcast(BF16) for _ in range(SPAN_TILES)] for _ in range(2)]
        x_parts = table_flat[:, 0:BLOCKS * 3 * F // 2].bitcast(BF16).rearrange("p (b k f) -> p b k f", b=BLOCKS, k=3)

        xn = sb("xn", [P, BLOCKS, F])
        acc = sb("acc", [P, BLOCKS + 2, F])
        rel_parts = [slots_flat[:, 0:RELS * F], slots_flat[:, RELS * F:2 * RELS * F],
                     acc[:, 0:BLOCKS // 2, :].rearrange("p b f -> p (b f)").bitcast(BF16)]
        cen = table_out[:, 0, :].rearrange("p (b f) -> p b f", f=F)
        sq = table_out[:, 1, :].rearrange("p (b f) -> p b f", f=F)
        st1 = sb("st1", [P, BLOCKS])
        st2 = sb("st2", [P, BLOCKS])
        st3 = sb("st3", [P, BLOCKS])

        psum = ctx.enter_context(nc.psum_tensor("psum", [P, 8, 512], F32))
        pair = [psum[:, 2 * k:2 * k + 2, :].rearrange("p a b -> p (a b)") for k in range(2)]
        bank_t = psum[:, 4, :]
        bank_h = [psum[:, 5, :], psum[:, 6, :]]
        bank_s = psum[:, 7, :]

        loaded = sem("loaded")
        x_loaded = sem("x_loaded")
        rel_loaded = sem("rel_loaded")
        iota_done = sem("iota_done")
        setup = sem("setup")
        ident_done = sem("ident_done")
        turned = sem("turned")
        keys_ready = sem("keys_ready")
        meta_ready = sem("meta_ready")
        split = sem("split")
        x_staged = sem("x_staged")
        x_turned = sem("x_turned")
        xT_ready = sem("xT_ready")
        table_mm = sem("table_mm")
        copied = [sem("copied_0"), sem("copied_1")]
        table_stored = [[sem(f"table_stored_{h}_{k}") for k in range(2)] for h in range(2)]
        rows_in = [[sem(f"rows_in_{l}_{s}") for s in range(SLOTS)] for l in range(4)]
        onehot_ready = [sem(f"onehot_ready_{l}") for l in range(4)]
        scattered = [sem(f"scattered_{l}") for l in range(4)]
        added = [sem(f"added_{l}") for l in range(4)]
        windows_done = [sem(f"windows_done_{l}") for l in range(4)]
        squared = sem("squared")
        weighted = sem("weighted")
        slot_freed = sem("slot_freed")
        sq_done = sem("sq_done")
        std_done = sem("std_done")
        x_ready = sem("x_ready")
        rows_out = [sem(f"rows_out_{l}") for l in range(4)]
        idx_in = [sem(f"idx_in_{s}") for s in range(SLOTS)]
        tiles_in = sem("tiles_in")
        split_ready = sem("split_ready")
        tiles_turned = sem("tiles_turned")
        tiles_T = sem("tiles_T")
        spans = sem("spans")
        span_turn = sem("span_turn")
        span_rows = sem("span_rows")
        ranges_ready = sem("ranges_ready")
        pairs_ready = sem("pairs_ready")
        span_done = sem("span_done")
        span_out = sem("span_out")
        counts_stored = sem("counts_stored")
        counts_loaded = [sem("counts_loaded_0"), sem("counts_loaded_1")]
        parts_ready = sem("parts_ready")
        block_sums = sem("block_sums")
        block_taken = sem("block_taken")
        zeroed = sem("zeroed")
        w3_loaded = sem("w3_loaded")
        w3_ready = sem("w3_ready")
        self_made = sem("self_made")
        self_added = sem("self_added")
        edges_in = [sem(f"edges_in_{s}") for s in range(SLOTS)]
        edges_turned = sem("edges_turned")
        edge_T_ready = sem("edge_T_ready")
        hidden_made = sem("hidden_made")
        hidden_ready = sem("hidden_ready")
        z_scaled = sem("z_scaled")
        z_free = sem("z_free")
        w_made = sem("w_made")
        pair_free = sem("pair_free")
        cprod_ready = sem("cprod_ready")
        c_ready = sem("c_ready")
        a_ready = sem("a_ready")
        pq_ready = sem("pq_ready")
        q_ready = sem("q_ready")
        half_a = sem("half_a")
        half_v = sem("half_v")
        folds = sem("folds")
        msg_ready = sem("msg_ready")
        folded_ready = sem("folded_ready")
        extra = {n: sem("extra_" + n) for n in ("window", "whole", "mod", "mod1", "moved", "reached", "key", "onehot", "scattered",
                                                 "fold", "folded", "added")}

        edge_cols = lambda a: a.rearrange("(c p j) -> p c j", p=P, j=TILES)
        node_rows = lambda a: a.rearrange("(b p) f -> p b f", p=P)
        cols3 = lambda t: t[:, :].rearrange("p (c j) -> p c j", j=TILES)

        edge_rows = edge_attr_32.rearrange("(c p j) f -> c p (j f)", p=P, j=TILES)
        sh_rows = edge_attr_4.rearrange("(c p j) f -> c p (j f)", p=P, j=TILES)
        W3_LOADS = 16 * (4 * 5 + 3)

        def numbers_at(eng, ap, least, most):
            return nc.values_load_multi_w_load_instructions(
                ap, [eng.engine], min_val=least, max_val=most,
                skip_runtime_bounds_check_because="worked out on the chip within these bounds")[1]

        def blocks_of(eng, c):
            return numbers_at(eng, meta[0:1, bass.ds(c, 1), :].rearrange("a c k -> a (c k)"), 0, BLOCKS)

        def is_dense(eng):
            return numbers_at(eng, dense_ok[0:1, 0:1], 0, 1)[0]

        block = ctx.enter_context(nc.Block())

        @block.sync
        def _(sp):
            sp.dma_start(xn[:, :, :], node_rows(x)).then_inc(x_loaded, 16)
            for q in range(4):
                sp.dma_start(rel_w[F * q:F * q + F, :].rearrange("i (r o) -> i r o", o=F),
                             L0_gnn_weight.rearrange("r i o -> i r o")).then_inc(rel_loaded, 16)
            sp.dma_start(cols3(dst_i), edge_cols(dst)).then_inc(loaded, 16)
            sp.dma_start(cols3(src_i), edge_cols(src)).then_inc(loaded, 16)
            sp.dma_start(cols3(key_i), edge_cols(edge_type_64)).then_inc(loaded, 16)
            sp.dma_start(cols3(weight), edge_cols(edge_weight)).then_inc(loaded, 16)

            by_tile = lambda a: a.rearrange("(k q e) -> q k e", q=P, e=P)
            sp.dma_start(src_r.rearrange("q (k e) -> q k e", e=P), by_tile(src)).then_inc(tiles_in, 16)
            sp.dma_start(dst_r.rearrange("q (k e) -> q k e", e=P), by_tile(dst)).then_inc(tiles_in, 16)

            sp.wait_ge(zeroed, 1)
            for q in range(4):
                sp.dma_start(w1[F * q:F * q + F, 0:HID], L3_gnn_W1).then_inc(w3_loaded, 16)
                sp.dma_start(w_self[F * q:F * q + MUL, 0:MUL], L3_gnn_si_w0).then_inc(w3_loaded, 16)
                for m in range(3):
                    sp.dma_start(w_self[F * q + MUL + m:F * q + F:3, MUL + m:F:3], L3_gnn_si_w1, allow_slow_non_contiguous=True
                                 ).then_inc(w3_loaded, 16)
            sp.dma_start(bias1[0:HID, :], L3_gnn_b1.rearrange("(h a) -> h a", a=1)).then_inc(w3_loaded, 16)
            sp.dma_start(w2_raw[0:HID, :], L3_gnn_W2).then_inc(w3_loaded, 16)
            sp.dma_start(w2_raw[HID:HID + 1, :], L3_gnn_b2.rearrange("(a n) -> a n", a=1)).then_inc(w3_loaded, 16)

            table_rows = rel_table.rearrange("(b p r) o -> b p (r o)", p=P, r=RELS)
            with sp.Fori(0, BLOCKS // 2) as it:
                for h in range(2):
                    for k in range(2):
                        half = slice(HALF * k, HALF * k + HALF)
                        sp.wait_ge(copied[k], it * 2 + (h + 1))
                        sp.dma_start(table_rows[bass.ds(it * 2 + h, 1), :, half].rearrange("b p c -> p (b c)"),
                                     table_out[:, h, half]).then_inc(table_stored[h][k], 16)

            sp.wait_ge(spans, SPAN_MM)
            sp.dma_start(tile_row.rearrange("p (k q) -> p k q", q=P), tile_mmT[:, :]).then_inc(span_rows, 16)

            def stage(l):
                numbers = key_i if l == 0 else src_i
                with sp.Fori(0, ROUNDS) as it:
                    for s in range(SLOTS):
                        c = it * SLOTS + s
                        sp.wait_ge(slot_freed, it * SLOTS + (l * CHUNKS + s + 1))
                        sp.dma_start(idx[:, s, :], numbers[:, bass.ds(it * (SLOTS * TILES) + s * TILES, TILES)]
                                     ).then_inc(idx_in[s], 16)
                        if l == 3:
                            sp.dma_start(edge_in[:, s, :, :].rearrange("p j f -> p (j f)"),
                                         edge_rows[bass.ds(c, 1), :, :].rearrange("c p k -> p (c k)")
                                         ).then_inc(edges_in[s], 16)
                            sp.dma_start(sh[:, s, :, :].rearrange("p j f -> p (j f)"),
                                         sh_rows[bass.ds(c, 1), :, :].rearrange("c p k -> p (c k)")
                                         ).then_inc(edges_in[s], 16)

            sp.wait_ge(keys_ready, 1)
            stage(0)
            stage(1)
            sp.wait_ge(ranges_ready, 1)
            dense = is_dense(sp)
            with sp.If(dense):
                sp.wait_ge(counts_stored, 16 * BLOCKS)
                for h in range(2):
                    sp.dma_start(counts_in[h], counts[h]).then_inc(counts_loaded[h], 16)
                with sp.Fori(1, BLOCKS // 2) as it:
                    for h in range(2):
                        sp.wait_ge(block_sums, it * 2 + (h - 1))
                        sp.dma_start(counts_in[h], counts[bass.ds(it * 2 + h, 1), :, :].rearrange("b p n -> p (b n)")
                                     ).then_inc(counts_loaded[h], 16)
            with sp.Else():
                stage(2)
            stage(3)

        @block.gpsimd
        def _(pool):
            pool.iota(iota_i[:, :], [[1, P]], base=1, channel_multiplier=0).then_inc(iota_done, 1)
            pool.iota(part_i[:, :], [[1, 1]], base=0, channel_multiplier=1).then_inc(iota_done, 1)
            pool.iota(tile_no_i, [[1, COLS]], base=1, channel_multiplier=0).then_inc(iota_done, 1)
            pool.iota(limits_i[:, :], [[P * SPAN, KS]], base=0, channel_multiplier=SPAN).then_inc(iota_done, 1)

            linked = [0]

            def part(ins):
                linked[0] += 1
                ins.then_inc(split, 1)
                pool.wait_ge(split, linked[0])

            pool.wait_ge(x_loaded, 16)
            left = cen
            part(pool.tensor_copy(node_parts[:, :, 0, :], xn[:, :, :]))
            part(pool.tensor_copy(node_parts[:, :, 3, :], xn[:, :, :]))
            part(pool.tensor_tensor(left, xn[:, :, :], node_parts[:, :, 0, :], ALU.subtract))
            part(pool.tensor_copy(node_parts[:, :, 1, :], left))
            part(pool.tensor_tensor(left, left, node_parts[:, :, 1, :], ALU.subtract))
            part(pool.tensor_copy(node_parts[:, :, 2, :], left))
            assert linked[0] == SPLIT_X

            for h in range(2):
                for k in range(2):
                    pool.wait_ge(table_stored[h][k], 16 * (BLOCKS // 2))
            due = [pool.alloc_register(f"idx_due_{s}") for s in range(SLOTS)]
            for s in range(SLOTS):
                pool.reg_mov(due[s], 16)
            def gather(l):
                if l >= 1:
                    pool.wait_ge(rows_out[l - 1], 16)
                with pool.Fori(0, ROUNDS) as it:
                    for s in range(SLOTS):
                        pool.wait_ge(idx_in[s], pool.snap(due[s]))
                        pool.reg_add(due[s], due[s], 16)
                        for j in range(TILES):
                            pool.indirect_dma_start(
                                gathered[:, s, j, :], None, rows[l],
                                bass.IndirectOffsetOnAxis(ap=idx[:, s, j:j + 1], axis=0),
                            ).then_inc(rows_in[l][s], 16)

            gather(0)
            gather(1)
            dense = is_dense(pool)
            with pool.If(dense < 1):
                gather(2)
            gather(3)

        @block.scalar
        def _(act):
            def table_group(g):
                if g is not FIRST:
                    act.wait_ge(x_turned, g)
                act.copy(group_parts[:, :], node_parts[:, bass.ds(g * 4, 4), :, :].rearrange("p b k f -> p (b k f)")
                         ).then_inc(x_staged, 1)
                act.wait_ge(x_turned, g + 1)
                if g is not FIRST:
                    act.wait_ge(table_mm, g * 8)
                act.copy(group_parts_T[:, :], bank_t).then_inc(xT_ready, 1)
                for q in range(4):
                    h = q % 2
                    for k in range(2):
                        act.wait_ge(table_mm, g * 8 + (2 * q + k + 1))
                        if g is not FIRST or q >= 2:
                            act.wait_ge(table_stored[h][k], g * 32 + 16 * (q // 2))
                        act.copy(table_out[:, h, HALF * k:HALF * k + HALF], pair[k]).then_inc(copied[k], 1)

            act.wait_ge(split, SPLIT_X)
            table_group(FIRST)
            with act.Fori(1, BLOCKS // 4) as g:
                table_group(g)

            def normalise(l):
                act.wait_ge(sq_done, 2 * l + 1)
                act.activation(sq[:, :, :], cen[:, :, :], ACT.Square).then_inc(sq_done, 1)
                act.wait_ge(std_done, 2 * l + 1)
                act.activation(st2[:, :], st1[:, :], ACT.Sqrt, bias=epsc[:, :], scale=1.0 / F).then_inc(std_done, 1)
                act.wait_ge(x_ready, l + 1)
                act.dma_start(node_rows(out if l == 3 else rows[l + 1]), xn[:, :, :]).then_inc(rows_out[l], 16)

            for n, to in ((0, pair_T), (1, low_T)):
                act.wait_ge(tiles_turned, n + 1)
                act.copy(to.rearrange("p (a b) -> p a b", b=512), psum[:, 4 * n:4 * n + 4, :]).then_inc(tiles_T, 1)
            act.wait_ge(spans, SPAN_FL)
            act.dma_start(range_f.rearrange("p (k q) -> p k q", q=P), first_lastT[:, :]).then_inc(span_rows, 16)

            def onehots(l, c, s):
                act.wait_ge(windows_done[l], c + 1)
                for j in range(TILES):
                    a = act.activation(onehot[:, s % 2, j, :], iota1[:, :], ACT.Square, scale=-1.0,
                                       bias=key_all[:, bass.ds(c * TILES + j, 1)])
                a.then_inc(squared, 1)
                act.wait_ge(squared, act.snap(squares))
                act.reg_add(squares, squares, 1)
                act.activation(onehot[:, s % 2, :, :], onehot[:, s % 2, :, :], ACT.Relu, scale=-1.0, bias=one_col[:, :]
                               ).then_inc(onehot_ready[l], 1)

            squares = act.alloc_register("act_squares")
            act.reg_mov(squares, 1)
            act.wait_ge(ranges_ready, 1)
            for l in range(2):
                with act.Fori(0, ROUNDS) as it:
                    for s in range(SLOTS):
                        onehots(l, it * SLOTS + s, s)
                        for i in range(PER_CHUNK):
                            n = s * PER_CHUNK + i
                            act.wait_ge(span_done, it * PER_BLOCK + (l * ROUNDS * PER_BLOCK + n + 3))
                            act.copy(counts_out.rearrange("p (h d) -> p d h", d=P)[:, SPAN * n:SPAN * n + SPAN, :],
                                         psum[:, i, :].rearrange("p (d h) -> p d h", d=SPAN)
                                         ).then_inc(span_out, 1)
                    act.wait_ge(span_out, it * PER_BLOCK + ((l * ROUNDS + 1) * PER_BLOCK + PER_CHUNK))
                    act.dma_start(counts[bass.ds(it + l * ROUNDS, 1), :, :].rearrange("b p n -> p (b n)"), counts_out
                                  ).then_inc(counts_stored, 16)
                    act.wait_ge(counts_stored, it * 16 + 16 * (l * ROUNDS + 1))
                normalise(l)
            dense = is_dense(act)
            with act.If(dense < 1):
                with act.Fori(0, ROUNDS) as it:
                    for s in range(SLOTS):
                        onehots(2, it * SLOTS + s, s)
            normalise(2)

            with act.Fori(0, BLOCKS // 4) as g:
                act.wait_ge(x_turned, g + BLOCKS // 4)
                act.copy(group_x[:, :], xn[:, bass.ds(g * 4, 4), :].rearrange("p b f -> p (b f)")
                         ).then_inc(x_staged, 1)
                act.wait_ge(x_turned, g + (BLOCKS // 4 + 1))
                act.wait_ge(self_made, g + 1)
                act.copy(group_xT[:, :], bank_t[:, 0:P]).then_inc(xT_ready, 1)

            def hidden_units(c, s):
                act.wait_ge(edges_turned, c + 1)
                act.wait_ge(hidden_made, c * GROUP + 1)
                act.copy(edge_T[:, :], bank_t).then_inc(edge_T_ready, 1)
                for q in range(GROUP):
                    act.wait_ge(hidden_made, c * GROUP + (q + 2))
                    if q == 0:
                        act.wait_ge(w_made, c * GROUP + GROUP)
                    act.activation(hidden[:, s % 2, q, :], bank_h[q % 2][0:HID + 1, :], ACT.Relu,
                                   bias=bias1[:, :]).then_inc(hidden_ready, 1)

            def scale_rows(c, s, it):
                act.wait_ge(rows_in[3][s], it * (16 * TILES) + 16 * TILES)
                act.wait_ge(edges_in[s], it * 32 + 32)
                act.wait_ge(z_free, c + 1)
                for j in range(TILES):
                    a = act.activation(z[:, s % 2, j, MUL:], gathered[:, s, j, :], ACT.Copy,
                                       scale=sh[:, s, j, 0:1])
                a.then_inc(z_scaled, 1)

            def beside(c, s, it, following=True):
                if following:
                    hidden_units(c + 1, s + 1)
                    scale_rows(c + 1, (s + 1) % SLOTS, it if s + 1 < SLOTS else it + 1)
                onehots(3, c, s)

            act.wait_ge(w3_ready, 1)
            hidden_units(0, 0)
            scale_rows(0, 0, 0)
            with act.Fori(0, ROUNDS - 1) as it:
                for s in range(SLOTS):
                    beside(it * SLOTS + s, s, it)
            for s in range(SLOTS):
                beside(CHUNKS - SLOTS + s, s, ROUNDS - 1, following=s + 1 < SLOTS)
            normalise(3)
            act.wait_ge(rows_out[3], 16)

        @block.tensor
        def _(pe):
            pe.wait_ge(ident_done, 1)
            pe.wait_ge(setup, SETUP_REL)
            def table_group(g):
                pe.wait_ge(x_staged, g + 1)
                if g is not FIRST:
                    pe.wait_ge(xT_ready, g)
                for q in range(4):
                    t = pe.transpose(bank_t[:, P * q:P * q + P], group_parts[:, P * q:P * q + P], ident[:, :])
                t.then_inc(x_turned, 1)
                pe.wait_ge(xT_ready, g + 1)
                for q in range(4):
                    for k in range(2):
                        if g is not FIRST or q > 0:
                            pe.wait_ge(copied[k], g * 4 + q)
                        for n in range(2):
                            for i, rows_used in enumerate(PASS_ROWS):
                                mm = pe.matmul(pair[k][:, 512 * n:512 * n + 512],
                                               group_parts_T[0:rows_used, P * q:P * q + P],
                                               rel_parts[i][0:rows_used, HALF * k + 512 * n:HALF * k + 512 * n + 512],
                                               start=(i == 0), stop=(i == 2))
                        mm.then_inc(table_mm, 1)

            table_group(FIRST)

            pe.wait_ge(setup, SETUP_MINMAX)
            pe.transpose(psum[:, 5, 0:P], dst_min[:, :], ident[:, :]).then_inc(turned, 1)
            pe.transpose(psum[:, 6, 0:P], dst_max[:, :], ident[:, :]).then_inc(turned, 1)
            pe.wait_ge(setup, SETUP_COL)
            pe.transpose(psum[0:1, 5, 0:P], col_min[:, 0:1], ident[:, :]).then_inc(turned, 1)
            pe.transpose(psum[0:1, 6, 0:P], col_min[:, 1:2], ident[:, :]).then_inc(turned, 1)
            pe.wait_ge(setup, SETUP_ROW)
            pe.matmul(psum[:, 5, 0:P], ones[:, :], row_min[0:1, 0, :], start=True, stop=True).then_inc(turned, 1)

            with pe.Fori(1, BLOCKS // 4) as g:
                table_group(g)

            pe.wait_ge(split_ready, 1)
            pe.wait_ge(copied[0], BLOCKS)
            pe.wait_ge(copied[1], BLOCKS)
            for n, what in ((0, pair_r), (1, low_r)):
                for k in range(KT):
                    t = pe.transpose(psum[:, 4 * n + k // 4, P * (k % 4):P * (k % 4) + P], what[:, P * k:P * k + P],
                                     ident[:, :])
                t.then_inc(tiles_turned, 1)
            pe.wait_ge(tiles_T, 2)
            pe.transpose(psum[0:2 * KT, 0, 0:P], tile_mm[:, :], ident[:, :]).then_inc(span_turn, 1)
            pe.wait_ge(span_rows, 16)
            for n in range(8):
                mm = pe.matmul(psum[:, n, :], ones[:, :], tile_row[:, 512 * n:512 * n + 512], start=True, stop=True)
            mm.then_inc(span_turn, 1)
            pe.wait_ge(spans, SPAN_LIMITS)
            pe.transpose(psum[0:2 * KS, 0, 0:P], first_last[:, :, :].rearrange("p a k -> p (a k)"), ident[:, :]
                         ).then_inc(span_turn, 1)

            def count_groups(n0):
                for i in range(PER_CHUNK):
                    pe.wait_ge(span_out, n0 + (i + 1))
                    pe.wait_ge(pairs_ready, n0 + (i + 1))
                    for k in range(SPAN_TILES):
                        mm = pe.matmul(psum[:, i, :], oh_low[i % 2][k], oh_pair[i % 2][k],
                                       start=(k == 0), stop=(k == SPAN_TILES - 1))
                    mm.then_inc(span_done, 1)

            pe.wait_ge(meta_ready, 1)
            pe.wait_ge(ranges_ready, 1)
            def scatter(l, s, tiles):
                for j in tiles:
                    message = msg[:, s % 2, j, :] if l == 3 else gathered[:, s, j, :]
                    mm = pe.matmul(bank_s[:, 0:message.shape[-1]], onehot[:, s % 2, j, :], message,
                                   start=(j == 0), stop=(j == TILES - 1))
                return mm

            extras = pe.alloc_register("pe_extras")
            pe.reg_mov(extras, 0)

            def scatter_extra(l, c, s):
                _, second_block, end_block = blocks_of(pe, c)
                with pe.If(second_block < end_block):
                    with pe.Fori(second_block, end_block):
                        n = pe.snap(extras)
                        pe.wait_ge(extra["onehot"], n + 1)
                        pe.wait_ge(added[l], c + 2)
                        scatter(l, s, range(TILES)).then_inc(extra["scattered"], 1)
                        pe.wait_ge(extra["added"], n + 1)
                        pe.reg_add(extras, extras, 1)

            def scatter_chunk(l, c, s, rows_due):
                pe.wait_ge(rows_in[l][s], rows_due)
                if l == 1:
                    pe.wait_ge(weighted, c + 1)
                pe.wait_ge(onehot_ready[l], c + 1)
                pe.wait_ge(added[l], c + 1)
                scatter(l, s, range(TILES)).then_inc(scattered[l], 1)

            def scatter_layer(l):
                for s in range(SLOTS):
                    if s > 0:
                        scatter_chunk(l, s - 1, s - 1, 16 * TILES)
                    if l < 2:
                        count_groups(l * ROUNDS * PER_BLOCK + s * PER_CHUNK)
                    if s > 0:
                        scatter_extra(l, s - 1, s - 1)
                with pe.Fori(1, ROUNDS) as it:
                    for s in range(SLOTS):
                        scatter_chunk(l, it * SLOTS + (s - 1), (s - 1) % SLOTS,
                                      it * (16 * TILES) + 16 * TILES if s > 0 else it * (16 * TILES))
                        if l < 2:
                            count_groups(it * PER_BLOCK + (l * ROUNDS * PER_BLOCK + s * PER_CHUNK))
                        scatter_extra(l, it * SLOTS + (s - 1), (s - 1) % SLOTS)
                scatter_chunk(l, CHUNKS - 1, SLOTS - 1, 16 * TILES * ROUNDS)
                scatter_extra(l, CHUNKS - 1, SLOTS - 1)

            scatter_layer(0)
            scatter_layer(1)
            dense = is_dense(pe)
            with pe.If(dense):
                with pe.Fori(0, BLOCKS // 2) as it:
                    for h in range(2):
                        pe.wait_ge(parts_ready, 1)
                        pe.wait_ge(counts_loaded[h], it * 16 + 16)
                        pe.wait_ge(block_taken, it * 2 + (h + 1))
                        for k in range(BLOCKS):
                            mm = pe.matmul(psum[:, 4 + h, 0:3 * F], counts_in[h][:, P * k:P * k + P],
                                           x_parts[:, k, :, :].rearrange("p k f -> p (k f)"),
                                           start=(k == 0), stop=(k == BLOCKS - 1))
                        mm.then_inc(block_sums, 1)
            with pe.Else():
                scatter_layer(2)

            pe.wait_ge(w3_ready, 1)
            with pe.Fori(0, BLOCKS // 4) as g:
                pe.wait_ge(x_staged, g + (BLOCKS // 4 + 1))
                pe.wait_ge(xT_ready, g + BLOCKS // 4)
                pe.transpose(bank_t[:, 0:P], group_x[:, :], ident[:, :]).then_inc(x_turned, 1)
                pe.wait_ge(xT_ready, g + (BLOCKS // 4 + 1))
                pe.wait_ge(self_added, g + 1)
                for q in range(4):
                    mm = pe.matmul(psum[:, q, 0:F], group_xT[F * q:F * q + F, :], w_self[F * q:F * q + F, :],
                                   start=True, stop=True, tile_position=(F * q, 0))
                mm.then_inc(self_made, 1)
            pe.wait_ge(self_added, BLOCKS // 4 + 1)

            def turn_edges(c, s, it):
                pe.wait_ge(edges_in[s], it * 32 + 32)
                pe.wait_ge(edge_T_ready, c + 1)
                for g in range(GROUP):
                    t = pe.transpose(bank_t[:, P * g:P * g + P],
                                     edge_in[:, s, GROUP * g:GROUP * g + GROUP, :].rearrange("p j f -> p (j f)"),
                                     ident[:, :])
                t.then_inc(edges_turned, 1)

            def hidden_units(c):
                pe.wait_ge(edge_T_ready, c + 2)
                for q in range(GROUP):
                    pe.wait_ge(hidden_ready, c * GROUP + (q + 1))
                    pe.matmul(bank_h[q % 2][0:HID + 1, :], w1[F * q:F * q + F, :], edge_T[F * q:F * q + F, :],
                              start=True, stop=True, tile_position=(F * q, 0)).then_inc(hidden_made, 1)

            def edge_weights(c, s, g):
                if g == 0:
                    pe.wait_ge(hidden_ready, c * GROUP + (GROUP + 2))
                pe.wait_ge(pair_free, c * GROUP + (g + 1))
                for q in range(GROUP):
                    mm = pe.matmul(pair[g % 2][:, WN * q:WN * q + WN], hidden[:, s % 2, q, P * g:P * g + P], w2[:, :],
                                   start=True, stop=True)
                mm.then_inc(w_made, 1)

            def chunk3(c, s, it, prev=True, following=True):
                if following:
                    turn_edges(c + 1, (s + 1) % SLOTS, it if s + 1 < SLOTS else it + 1)
                for g in range(GROUP):
                    edge_weights(c, s, g)
                    if g == 0 and following:
                        hidden_units(c + 1)
                    if prev and g >= 1:
                        if g == 1:
                            pe.wait_ge(onehot_ready[3], c)
                            pe.wait_ge(msg_ready, c * GROUP + 1)
                            pe.wait_ge(added[3], c)
                        mm = scatter(3, (s - 1) % SLOTS, (range(5), range(5, 11), range(11, TILES))[g - 1])
                if prev:
                    mm.then_inc(scattered[3], 1)
                    scatter_extra(3, c - 1, (s - 1) % SLOTS)

            turn_edges(0, 0, 0)
            hidden_units(0)
            for s in range(SLOTS):
                chunk3(s, s, 0, prev=s > 0)
            with pe.Fori(1, ROUNDS - 1) as it:
                for s in range(SLOTS):
                    chunk3(it * SLOTS + s, s, it)
            for s in range(SLOTS):
                chunk3(CHUNKS - SLOTS + s, s, ROUNDS - 1, following=s + 1 < SLOTS)
            pe.wait_ge(onehot_ready[3], CHUNKS)
            pe.wait_ge(msg_ready, CHUNKS * GROUP + 1)
            pe.wait_ge(added[3], CHUNKS)
            scatter(3, SLOTS - 1, range(TILES)).then_inc(scattered[3], 1)
            scatter_extra(3, CHUNKS - 1, SLOTS - 1)

        @block.vector
        def _(dve):
            chain = [0]

            def link(ins):
                chain[0] += 1
                ins.then_inc(setup, 1)
                dve.wait_ge(setup, chain[0])

            dve.memset(ones[:, :], 1.0)
            dve.memset(epsc[:, :], 1e-5)
            dve.memset(one_col[:, :], 1.0)
            dve.memset(w1[:, :], 0.0)
            dve.memset(bias1[:, :], 1.0)
            dve.memset(w_self[:, :], 0.0).then_inc(zeroed, 1)
            for start, n in ((slot_freed, SLOTS), (z_free, 2), (pair_free, 2), (hidden_ready, 2), (hidden_made, 1),
                             (edge_T_ready, 1), (self_made, 1), (self_added, 1), (w_made, 2 * GROUP),
                             (msg_ready, 1), (q_ready, 1), (half_a, 1), (half_v, 1), (span_done, 2),
                             (span_out, PER_CHUNK), (block_taken, 2), *((a, 1) for a in added),
                             *((w, 2) for w in windows_done)):
                dve.sem_inc(start, n)
            dve.wait_ge(rel_loaded, 64)
            top = slice(0, 3 * F)
            link(dve.tensor_copy(rel_parts[0], rel_w[:, :]))
            link(dve.tensor_tensor(rel_w[:, :], rel_w[:, :], rel_parts[0], ALU.subtract))
            dve.tensor_copy(rel_parts[0][3 * F:P], rel_w[3 * F:P, :])
            link(dve.tensor_copy(rel_parts[1][top], rel_w[top, :]))
            link(dve.tensor_tensor(rel_w[top, :], rel_w[top, :], rel_parts[1][top], ALU.subtract))
            dve.tensor_copy(rel_parts[1][0:F], rel_w[0:F, :])
            link(dve.tensor_copy(rel_parts[2][top], rel_w[top, :]))
            link(dve.memset(rel_parts[2][0:F], 0.0))
            assert chain[0] == SETUP_REL, chain[0]
            dve.wait_ge(iota_done, 4)
            link(dve.tensor_copy(iota1[:, :], iota_i[:, :]))
            link(dve.tensor_copy(part[:, :], part_i[:, :]))
            link(dve.tensor_scalar(part1[:, :], part[:, :], 1.0, None, ALU.add))
            dve.tensor_scalar(ident[:, :], iota1[:, :], part1[:, 0:1], None, ALU.is_equal).then_inc(ident_done, 1)
            dve.wait_ge(loaded, 64)
            link(dve.tensor_copy(dst_f[:, :], dst_i[:, :]))
            link(dve.tensor_scalar(dmod_i[:, :], dst_i[:, :], P - 1, None, ALU.bitwise_and))
            link(dve.tensor_scalar(key_all[:, :], dmod_i[:, :], 1.0, None, ALU.add))
            dve.scalar_tensor_tensor(key_i[:, :], src_i[:, :], float(RELS), key_i[:, :], ALU.mult,
                                     ALU.add).then_inc(keys_ready, 1)
            link(dve.tensor_reduce(dst_min[:, :], cols3(dst_f), AX.X, ALU.min))
            link(dve.tensor_reduce(dst_max[:, :], cols3(dst_f), AX.X, ALU.max))
            assert chain[0] == SETUP_MINMAX, chain[0]
            dve.wait_ge(turned, 2)
            link(dve.tensor_reduce(col_min[:, 0:1], psum[:, 5, 0:P], AX.X, ALU.min))
            link(dve.tensor_reduce(col_min[:, 1:2], psum[:, 6, 0:P], AX.X, ALU.max))
            assert chain[0] == SETUP_COL, chain[0]
            dve.wait_ge(turned, 4)
            link(dve.tensor_copy(row_min[0:1, 0, :], psum[0:1, 5, 0:P]))
            assert chain[0] == SETUP_ROW, chain[0]
            link(dve.tensor_tensor(row_min[0:1, 1, :], psum[0:1, 6, 0:P], row_min[0:1, 0, :], ALU.subtract))
            link(dve.tensor_copy(row_i[0:1, :, :], row_min[0:1, :, :]))
            link(dve.tensor_scalar(meta[0:1, :, 0:3:2].rearrange("a c k -> a k c"), row_i[0:1, :, :], 7, None,
                                   ALU.logical_shift_right))
            link(dve.tensor_scalar(meta[0:1, :, 1], meta[0:1, :, 0], 1.0, None, ALU.add))
            link(dve.scalar_tensor_tensor(meta[0:1, :, 2], meta[0:1, :, 2], 1.0, meta[0:1, :, 0], ALU.add, ALU.add))
            dve.wait_ge(turned, 5)
            link(dve.tensor_copy(base[:, :], psum[:, 5, 0:P]))
            link(dve.tensor_copy(base_i[:, :], base[:, :]))
            link(dve.tensor_scalar(base_i[:, :], base_i[:, :], P - 1, None, ALU.bitwise_and))
            link(dve.tensor_copy(basemod[:, :], base_i[:, :]))
            link(dve.tensor_scalar(in_first[:, :], basemod[:, :], part[:, 0:1], None, ALU.is_le))
            link(dve.tensor_scalar(in_next[:, :], basemod[:, :], part[:, 0:1], None, ALU.is_gt))
            link(dve.tensor_scalar(base_end[:, :], base[:, :], float(P), None, ALU.add))
            link(dve.tensor_tensor(cols3(tile_back), cols3(dst_f),
                                   base_end[:, :].unsqueeze(2).to_broadcast([P, CHUNKS, TILES]), ALU.is_lt))
            link(dve.tensor_tensor(key_all[:, :], key_all[:, :], tile_back, ALU.mult))
            dve.sem_inc(meta_ready, 1)

            dve.wait_ge(tiles_in, 32)
            link(dve.tensor_scalar(high_r, src_r, 7, None, ALU.logical_shift_right))
            link(dve.tensor_scalar(src_r, src_r, P - 1, None, ALU.bitwise_and))
            link(dve.tensor_copy(low_r, src_r))
            link(dve.scalar_tensor_tensor(pair_r, dst_r, float(BLOCKS), high_r, ALU.mult, ALU.add))
            link(dve.tensor_reduce(tile_mm[:, 0:KT], dst_r.rearrange("q (k e) -> q k e", e=P), AX.X, ALU.min))
            link(dve.tensor_reduce(tile_mm[:, KT:2 * KT], dst_r.rearrange("q (k e) -> q k e", e=P), AX.X, ALU.max))
            dve.sem_inc(split_ready, 1)
            link(dve.tensor_copy(tile_no, tile_no_i))
            link(dve.tensor_scalar(tile_back, tile_no, -1.0, COLS + 1.0, ALU.mult, ALU.add))
            link(dve.tensor_scalar(iota_span[:, :], tile_no[:, 0:SPAN_COLS], -1.0, None, ALU.add))
            link(dve.tensor_scalar(span_base[:, :], tile_no[:, 0:SPANS], -1.0, float(SPAN_COLS), ALU.add, ALU.mult))
            link(dve.tensor_copy(limits[:, 0, :], limits_i[:, :]))
            link(dve.tensor_scalar(limits[:, 1, :], limits[:, 0, :], SPAN - 1.0, None, ALU.add))

            dve.wait_ge(w3_loaded, W3_LOADS)
            raw = w2_raw[:, :].rearrange("h (k i o) -> h k o i", k=4, i=MUL)
            w2_a = w2[:, 0:A_END].rearrange("h (o k i) -> h k o i", o=MUL, k=2)
            oi = lambda ap: ap.rearrange("h (o i) -> h o i", o=MUL)
            dve.tensor_scalar(w2_a[:, 0], raw[:, 3], C110, None, ALU.mult)
            dve.tensor_copy(w2_a[:, 1], raw[:, 0])
            dve.tensor_copy(oi(w2[:, A_END:Q_END]), raw[:, 1])
            dve.tensor_copy(oi(w2[:, Q_END:WN]), raw[:, 2]).then_inc(w3_ready, 1)

            def normalise(l):
                if l >= 1:
                    dve.wait_ge(rows_out[l - 1], 16)
                if l == 3:
                    link(dve.scalar_tensor_tensor(xn[:, :, :], acc[:, 0:BLOCKS, :], ALPHA, xn[:, :, :],
                                                  ALU.mult, ALU.add))
                else:
                    link(dve.tensor_tensor(xn[:, :, :], xn[:, :, :], acc[:, 0:BLOCKS, :], ALU.add))
                link(dve.tensor_reduce(st1[:, :], xn[:, :, :], AX.X, ALU.add))
                link(dve.tensor_scalar(st1[:, :], st1[:, :], 1.0 / F, None, ALU.mult))
                dve.tensor_tensor(cen[:, :, :], xn[:, :, :], st1[:, :].unsqueeze(2).to_broadcast([P, BLOCKS, F]),
                                  ALU.subtract).then_inc(sq_done, 1)
                if l < 2:
                    link(dve.memset(acc[:, :, :], 0.0))
                dve.wait_ge(sq_done, 2 * l + 2)
                dve.tensor_reduce(st1[:, :], sq[:, :, :], AX.X, ALU.add).then_inc(std_done, 1)
                dve.wait_ge(std_done, 2 * l + 2)
                link(dve.reciprocal(st3[:, :], st2[:, :]))
                dve.tensor_tensor(xn[:, :, :], cen[:, :, :], st3[:, :].unsqueeze(2).to_broadcast([P, BLOCKS, F]),
                                  ALU.mult).then_inc(x_ready, 1)

            dve.wait_ge(table_mm, 2 * BLOCKS)
            link(dve.memset(acc[:, :, :], 0.0))

            count = [0]

            def span_link(ins):
                count[0] += 1
                ins.then_inc(spans, 1)
                dve.wait_ge(spans, count[0])

            dve.wait_ge(span_turn, 1)
            span_link(dve.tensor_copy(tile_mmT[:, :], psum[0:2 * KT, 0, 0:P]))
            dve.wait_ge(span_turn, 2)
            all_tiles = lambda n: psum[:, 4 * n:4 * n + 4, :].rearrange("p a b -> p (a b)")
            for k in range(KS):
                span_link(dve.scalar_tensor_tensor(masked, all_tiles(1), limits[:, 0, k:k + 1], tile_back,
                                                   ALU.is_ge, ALU.mult))
                span_link(dve.tensor_reduce(first_last[:, 0, k:k + 1], masked, AX.X, ALU.max))
                span_link(dve.scalar_tensor_tensor(masked, all_tiles(0), limits[:, 1, k:k + 1], tile_no,
                                                   ALU.is_le, ALU.mult))
                span_link(dve.tensor_reduce(first_last[:, 1, k:k + 1], masked, AX.X, ALU.max))
            span_link(dve.tensor_scalar(first_last[:, 0, :], first_last[:, 0, :], -1.0, float(COLS), ALU.mult, ALU.add))
            span_link(dve.tensor_scalar(first_last[:, 0, :], first_last[:, 0, :], float(COLS - SPAN_TILES), None,
                                        ALU.min))
            assert count[0] == SPAN_LIMITS
            dve.wait_ge(span_turn, 3)
            span_link(dve.tensor_copy(first_lastT[:, :], psum[0:2 * KS, 0, 0:P]))
            assert count[0] == SPAN_FL
            dve.wait_ge(span_rows, 32)
            length = row_space[:, 2 * SPANS:3 * SPANS]
            first_f, end_f = range_f[:, 0:SPANS], range_f[:, SPANS:2 * SPANS]
            span_link(dve.tensor_tensor(length, end_f, first_f, ALU.subtract))
            span_link(dve.tensor_reduce(span_stat[:, 0:1], length, AX.X, ALU.max))
            span_link(dve.tensor_scalar(span_stat[:, 1:2], span_stat[:, 0:1], float(SPAN_TILES), None, ALU.is_le))
            span_link(dve.tensor_copy(dense_ok[:, :], span_stat[:, 1:2]))
            span_link(dve.tensor_copy(firsts, first_f))
            dve.sem_inc(ranges_ready, 1)

            def count_groups(n0):
                first = numbers_at(dve, firsts[:, bass.ds(n0, PER_CHUNK)], 0, COLS - SPAN_TILES)
                for i in range(PER_CHUNK):
                    b = i % 2
                    dve.wait_ge(span_done, n0 + (i + 1))
                    for k in range(SPAN_TILES):
                        t = bass.ds(first[i] + k, 1)
                        dve.tensor_scalar(oh_low[b][k], iota_low, low_T[:, t], None, ALU.is_equal)
                        last = dve.tensor_scalar(oh_pair[b][k], iota_span[:, :], span_base[:, bass.ds(n0 + i, 1)],
                                                 pair_T[:, t], ALU.add, ALU.is_equal)
                    last.then_inc(pairs_ready, 1)

            extras = dve.alloc_register("dve_extras")
            dve.reg_mov(extras, 0)
            extra_chunks = dve.alloc_register("dve_extra_chunks")
            dve.reg_mov(extra_chunks, 0)

            def add_window(l, b0, c, before, fold, folded_sem, done):
                if l == 3:
                    dve.tensor_reduce(folded[:, 0:MUL], bank_s[:, 0:MA].rearrange("p (o i) -> p o i", o=MUL),
                                      AX.X, ALU.add)
                    dve.tensor_reduce(folded_q[:, :].rearrange("p (o m) -> p m o", m=3),
                                      bank_s[:, MQ:MSG].rearrange("p (m o i) -> p m o i", m=3, o=MUL), AX.X, ALU.add
                                      ).then_inc(fold, 1)
                    dve.wait_ge(fold, before + 1)
                    dve.tensor_tensor(folded[:, MUL:F], folded_q[:, :], bank_s[:, MA:MQ], ALU.add
                                      ).then_inc(folded_sem, 1)
                    dve.wait_ge(folded_sem, before + 1)
                sums = folded[:, :] if l == 3 else bank_s[:, 0:F]
                for n, part_of in ((0, in_first), (1, in_next)):
                    to = acc[:, bass.ds(b0 + n, 1), :].rearrange("p b f -> p (b f)")
                    last = dve.scalar_tensor_tensor(to, sums, part_of[:, bass.ds(c, 1)], to, ALU.mult, ALU.add)
                last.then_inc(done, 1)

            def add_chunk(l, c, s):
                first_block, second_block, end_block = blocks_of(dve, c)
                dve.wait_ge(scattered[l], c + 1)
                dve.wait_ge(added[l], c + 1)
                add_window(l, first_block, c, c, folds, folded_ready, added[l])
                with dve.If(second_block < end_block):
                    cols = bass.ds(c * TILES, TILES)
                    dve.wait_ge(added[l], c + 2)
                    dve.tensor_copy(window[:, :], base[:, bass.ds(c, 1)]).then_inc(extra["window"], 1)
                    dve.reg_add(extra_chunks, extra_chunks, 1)
                    nth = dve.snap(extra_chunks)
                    with dve.Fori(second_block, end_block) as b0:
                        n = dve.snap(extras)
                        dve.wait_ge(extra["window"], nth)
                        dve.tensor_copy(mod_i[:, :], dst_f[:, cols]).then_inc(extra["whole"], 1)
                        dve.tensor_scalar(window[:, :], window[:, :], float(P), None, ALU.add
                                          ).then_inc(extra["moved"], 1)
                        dve.wait_ge(extra["whole"], n + 1)
                        dve.tensor_scalar(mod_out[:, :], mod_i[:, :], P - 1, None, ALU.bitwise_and
                                          ).then_inc(extra["mod"], 1)
                        dve.wait_ge(extra["mod"], n + 1)
                        dve.tensor_scalar(mod1[:, :], mod_out[:, :], 1.0, None, ALU.add).then_inc(extra["mod1"], 1)
                        dve.wait_ge(extra["mod1"], n + 1)
                        dve.wait_ge(extra["moved"], n * 2 + 1)
                        dve.scalar_tensor_tensor(reached[:, :], dst_f[:, cols], window[:, 0:1], mod1[:, :],
                                                 ALU.is_ge, ALU.mult).then_inc(extra["reached"], 1)
                        dve.tensor_scalar(window_end[:, :], window[:, :], float(P), None, ALU.add
                                          ).then_inc(extra["moved"], 1)
                        dve.wait_ge(extra["reached"], n + 1)
                        dve.wait_ge(extra["moved"], n * 2 + 2)
                        dve.scalar_tensor_tensor(key[:, :], dst_f[:, cols], window_end[:, 0:1], reached[:, :],
                                                 ALU.is_lt, ALU.mult).then_inc(extra["key"], 1)
                        dve.wait_ge(extra["key"], n + 1)
                        dve.tensor_tensor(onehot[:, s % 2, :, :],
                                          iota1[:, :].unsqueeze(1).to_broadcast([P, TILES, P]),
                                          key[:, :].unsqueeze(2).to_broadcast([P, TILES, P]), ALU.is_equal
                                          ).then_inc(extra["onehot"], 1)
                        dve.wait_ge(extra["scattered"], n + 1)
                        add_window(l, b0, c, n, extra["fold"], extra["folded"], extra["added"])
                        if l < 3:
                            dve.sem_inc(extra["fold"], 1)
                            dve.sem_inc(extra["folded"], 1)
                        dve.wait_ge(extra["added"], n + 1)
                        dve.reg_add(extras, extras, 1)
                if l < 3:
                    dve.sem_inc(slot_freed, 1)
                dve.sem_inc(windows_done[l], 1)

            def scatter_layer(l):
                def weigh(c, s, rows_due):
                    dve.wait_ge(rows_in[l][s], rows_due)
                    dve.tensor_tensor(gathered[:, s, :, :], gathered[:, s, :, :],
                                      weight[:, bass.ds(c * TILES, TILES)].unsqueeze(2).to_broadcast([P, TILES, F]),
                                      ALU.mult).then_inc(weighted, 1)

                for s in range(SLOTS):
                    if l < 2:
                        count_groups(l * ROUNDS * PER_BLOCK + s * PER_CHUNK)
                    if l == 1:
                        weigh(s, s, 16 * TILES)
                    if s > 0:
                        add_chunk(l, s - 1, s - 1)
                with dve.Fori(1, ROUNDS) as it:
                    for s in range(SLOTS):
                        if l < 2:
                            count_groups(it * PER_BLOCK + (l * ROUNDS * PER_BLOCK + s * PER_CHUNK))
                        if l == 1:
                            weigh(it * SLOTS + s, s, it * (16 * TILES) + 16 * TILES)
                        add_chunk(l, it * SLOTS + (s - 1), (s - 1) % SLOTS)
                add_chunk(l, CHUNKS - 1, SLOTS - 1)
                dve.wait_ge(added[l], CHUNKS + 1)

            scatter_layer(0)
            normalise(0)
            scatter_layer(1)
            normalise(1)
            dense = is_dense(dve)
            with dve.If(dense):
                dve.wait_ge(x_ready, 2)
                link(dve.tensor_copy(x_parts[:, :, 0, :], xn[:, :, :]))
                link(dve.tensor_tensor(rest, xn[:, :, :], x_parts[:, :, 0, :], ALU.subtract))
                link(dve.tensor_copy(x_parts[:, :, 1, :], rest))
                link(dve.tensor_tensor(rest, rest, x_parts[:, :, 1, :], ALU.subtract))
                dve.tensor_copy(x_parts[:, :, 2, :], rest).then_inc(parts_ready, 1)
                with dve.Fori(0, BLOCKS // 2) as it:
                    for h in range(2):
                        dve.wait_ge(block_sums, it * 2 + (h + 1))
                        dve.tensor_reduce(acc[:, bass.ds(it * 2 + h, 1), :].rearrange("p b f -> p (b f)"),
                                          psum[:, 4 + h, 0:3 * F].rearrange("p (k f) -> p f k", k=3), AX.X, ALU.add
                                          ).then_inc(block_taken, 1)
                dve.wait_ge(block_taken, BLOCKS + 2)
                dve.sem_inc(slot_freed, CHUNKS)
            with dve.Else():
                scatter_layer(2)
                dve.sem_inc(setup, 4)
            normalise(2)

            link(dve.memset(acc[:, BLOCKS:, :], 0.0))
            with dve.Fori(0, BLOCKS // 4) as g:
                dve.wait_ge(self_made, g + 2)
                dve.tensor_scalar(acc[:, bass.ds(g * 4, 4), :], psum[:, 0:4, 0:F], SI_SCALE / ALPHA, None,
                                  ALU.mult).then_inc(self_added, 1)

            def messages(c, s, it):
                dve.wait_ge(rows_in[3][s], it * (16 * TILES) + 16 * TILES)
                dve.wait_ge(edges_in[s], it * 32 + 32)
                zs = z[:, s % 2]
                v = gathered[:, s, :, MUL:F].rearrange("p j (i m) -> p j i m", m=3)
                sh1 = sh[:, s, :, 1:4]
                dve.tensor_tensor(cprod[:, :, :, :], v, sh1.unsqueeze(2).to_broadcast([P, TILES, MUL, 3]), ALU.mult
                                  ).then_inc(cprod_ready, 1)
                dve.wait_ge(cprod_ready, c + 1)
                dve.tensor_reduce(zs[:, :, 0:MUL], cprod[:, :, :, :], AX.X, ALU.add).then_inc(c_ready, 1)
                dve.wait_ge(c_ready, c + 1)
                dve.wait_ge(z_scaled, c + 1)
                for g in range(GROUP):
                    tiles = slice(GROUP * g, GROUP * g + GROUP)
                    group = c * GROUP + g
                    w = pair[g % 2].rearrange("p (j n) -> p j n", n=WN)
                    over_o = lambda ap, n: ap.unsqueeze(2).to_broadcast([P, GROUP, MUL, n])
                    split = lambda ap, n: ap.rearrange("p j (o n) -> p j o n", n=n)
                    dve.wait_ge(w_made, c * GROUP + (g + 2 * GROUP + 1))
                    dve.wait_ge(q_ready, group + 1)
                    dve.tensor_tensor(prod_q[:, :, :, :], split(w[:, :, A_END:Q_END], MUL),
                                      over_o(gathered[:, s, tiles, 0:MUL], MUL), ALU.mult).then_inc(pq_ready, 1)
                    dve.wait_ge(half_a, group + 1)
                    dve.tensor_tensor(prod_a[:, :, :, :], split(w[:, :, 0:A_END], 2 * MUL),
                                      over_o(zs[:, tiles, 0:2 * MUL], 2 * MUL), ALU.mult).then_inc(a_ready, 1)
                    dve.wait_ge(half_v, group + 1)
                    for m in range(3):
                        last = dve.tensor_tensor(
                            prod_v[:, :, m], split(w[:, :, Q_END:WN], MUL),
                            over_o(zs[:, tiles, ZC + m:5 * MUL:3], MUL), ALU.mult)
                    last.then_inc(pair_free, 1)
                    to = msg[:, s % 2, tiles]
                    dve.wait_ge(pq_ready, group + 1)
                    dve.wait_ge(msg_ready, group + 1)
                    dve.tensor_reduce(q_sum[:, :, :], prod_q[:, :, :, :], AX.X, ALU.add).then_inc(q_ready, 1)
                    dve.wait_ge(a_ready, group + 1)
                    dve.tensor_tensor(split(to[:, :, 0:MA], MUL), prod_a[:, :, :, 0:MUL], prod_a[:, :, :, MUL:],
                                      ALU.add).then_inc(half_a, 1)
                    dve.wait_ge(pair_free, group + 3)
                    half = prod_v[:, :, :, :, :].rearrange("p j m o i -> p j (m o) i")
                    dve.tensor_tensor(split(to[:, :, MQ:MSG], 4), half[:, :, :, 0:4], half[:, :, :, 4:8], ALU.add
                                      ).then_inc(half_v, 1)
                    dve.wait_ge(q_ready, group + 2)
                    dve.tensor_tensor(split(to[:, :, MA:MQ], 3),
                                      q_sum[:, :, :].unsqueeze(3).to_broadcast([P, GROUP, MUL, 3]),
                                      sh1[:, tiles].unsqueeze(2).to_broadcast([P, GROUP, MUL, 3]), ALU.mult
                                      ).then_inc(msg_ready, 1)

            def release(c):
                dve.wait_ge(msg_ready, c * GROUP + (GROUP + 1))
                dve.sem_inc(z_free, 1)
                dve.sem_inc(slot_freed, 1)

            messages(0, 0, 0)
            release(0)
            for s in range(1, SLOTS):
                messages(s, s, 0)
                add_chunk(3, s - 1, s - 1)
                release(s)
            with dve.Fori(1, ROUNDS) as it:
                for s in range(SLOTS):
                    messages(it * SLOTS + s, s, it)
                    add_chunk(3, it * SLOTS + (s - 1), (s - 1) % SLOTS)
                    release(it * SLOTS + s)
            add_chunk(3, CHUNKS - 1, SLOTS - 1)
            dve.wait_ge(added[3], CHUNKS + 1)
            normalise(3)
    return nc


_INS = ["x", "src", "dst", "edge_attr_32", "edge_attr_4", "edge_type_64", "edge_weight", "L0_gnn_weight",
        "L3_gnn_W1", "L3_gnn_b1", "L3_gnn_W2", "L3_gnn_b2", "L3_gnn_si_w0", "L3_gnn_si_w1"]


def kernel(**inputs):
    import numpy as np
    import concourse.bacc as bacc
    from concourse.bass_utils import run_bass_kernel_spmd

    nc = bacc.Bacc("TRN2", target_bir_lowering=False, num_devices=1)
    arrays, args = {}, []
    for name in _INS:
        a = np.ascontiguousarray(inputs[name])
        arrays[f"in_{name}"] = a
        args.append(nc.dram_tensor(f"in_{name}", a.shape, mybir.dt.from_np(a.dtype), kind="ExternalInput").ap())
    args.append(nc.dram_tensor("out", arrays["in_x"].shape, F32, kind="ExternalOutput").ap())
    build(nc, *args)
    return run_bass_kernel_spmd(nc, [arrays], core_ids=[0]).results[0]["out"]
```
